# Optimizing a Trainium2 kernel written in Bass

```python
import numpy as np
import jax
import jax.numpy as jnp

def _softmax(x, axis=-1):
    return jax.nn.softmax(x, axis=axis)

def _gelu(x):
    return jax.nn.gelu(x, approximate=True)

def _silu(x):
    return jax.nn.silu(x)

def _sigmoid(x):
    return jax.nn.sigmoid(x)

def _layernorm(x, axis=-1, eps=1e-05):
    m = jnp.mean(x, axis=axis, keepdims=True)
    v = jnp.var(x, axis=axis, keepdims=True)
    return (x - m) / jnp.sqrt(v + eps)

def _scatter_add(tgt, idx, src, axis=0):
    return tgt.at[idx].add(src)

def _segment_sum(src, seg, n):
    return jax.ops.segment_sum(src, seg, n)
kernel_name = 'mk_adaln_d1_jaxref_r4_cd5446'

def setup_inputs(seed: int=0):
    np.random.seed(seed)
    _w = jnp.asarray

    def _L0_attn_setup():
        import jax, jax.numpy as jnp
        import numpy as np
        N_EMBD = 256
        N_HEAD = 16
        HEAD_DIM = N_EMBD // N_HEAD
        KV_RANK = 64
        Q_RANK = 128
        ROPE_DIM = 32
        B, T = (2, 512)
        EPS = 1e-06

        def _rope_tables(T, dim):
            inv_freq = 1.0 / 10000.0 ** (np.arange(0, dim, 2, dtype=np.float32) / dim)
            t = np.arange(T, dtype=np.float32)
            freqs = np.outer(t, inv_freq)
            emb = np.concatenate([freqs, freqs], -1)
            return (jnp.asarray(np.cos(emb)), jnp.asarray(np.sin(emb)))

        def _apply_rope(x, cos, sin):
            d2 = x.shape[-1] // 2
            x1, x2 = (x[..., :d2], x[..., d2:])
            rot = jnp.concatenate([-x2, x1], axis=-1)
            return x * cos[None, None, :, :] + rot * sin[None, None, :, :]
        key = jax.random.key(seed)
        ks = jax.random.split(key, 10)

        def w(k, fan_in, fan_out):
            return jax.random.normal(k, (fan_in, fan_out), dtype=jnp.float32) * fan_in ** (-0.5)
        return {'x': jax.random.normal(ks[0], (B, T, N_EMBD), dtype=jnp.float32), 'W_kv': w(ks[1], N_EMBD, KV_RANK), 'g_kv': jnp.ones((KV_RANK,), dtype=jnp.float32), 'W_kdec': w(ks[2], KV_RANK, N_HEAD * HEAD_DIM), 'W_vdec': w(ks[3], KV_RANK, N_HEAD * HEAD_DIM), 'W_q': w(ks[4], N_EMBD, Q_RANK), 'W_qdec': w(ks[5], Q_RANK, N_HEAD * HEAD_DIM), 'W_krope': w(ks[6], N_EMBD, N_HEAD * ROPE_DIM), 'W_qrope': w(ks[7], Q_RANK, N_HEAD * ROPE_DIM), 'W_o': w(ks[8], N_HEAD * HEAD_DIM, N_EMBD)}
    _L0_attn_in = _L0_attn_setup()

    def _L0_ffn_setup():
        import jax, jax.numpy as jnp
        import numpy as np
        BS, L, D = (4, 512, 256)
        H, E, K = (8, 16, 2)
        HD = D // H
        I = 1024 // H
        key = jax.random.key(seed)
        ks = jax.random.split(key, 10)
        s = lambda k, shp, fan: jax.random.normal(k, shp, jnp.float32) / np.sqrt(fan)
        return {'x': jax.random.normal(ks[0], (BS, L, D), jnp.float32), 'Wm': s(ks[1], (D, D), D), 'bm': jnp.zeros((D,), jnp.float32), 'expert_emb': jax.random.normal(ks[2], (HD, E), jnp.float32), 'W1': s(ks[3], (E, HD, I), HD), 'b1': jnp.zeros((E, I), jnp.float32), 'W2': s(ks[4], (E, I, HD), I), 'b2': jnp.zeros((E, HD), jnp.float32), 'Wo': s(ks[5], (D, D), D), 'bo': jnp.zeros((D,), jnp.float32)}
    _L0_ffn_in = _L0_ffn_setup()
    _L0_c = _w((lambda *s: np.random.randn(*s).astype(np.float32) * 0.05)(8, 256))
    _L0_wmod = _w((lambda *s: np.random.randn(*s).astype(np.float32) * 0.05)(256, 6 * 256) * 256 ** (-0.5))
    _d = {'L0_attn_x': _L0_attn_in['x'], 'L0_attn_W_kv': _L0_attn_in['W_kv'], 'L0_attn_g_kv': _L0_attn_in['g_kv'], 'L0_attn_W_kdec': _L0_attn_in['W_kdec'], 'L0_attn_W_vdec': _L0_attn_in['W_vdec'], 'L0_attn_W_q': _L0_attn_in['W_q'], 'L0_attn_W_qdec': _L0_attn_in['W_qdec'], 'L0_attn_W_krope': _L0_attn_in['W_krope'], 'L0_attn_W_qrope': _L0_attn_in['W_qrope'], 'L0_attn_W_o': _L0_attn_in['W_o'], 'L0_ffn_Wm': _L0_ffn_in['Wm'], 'L0_ffn_bm': _L0_ffn_in['bm'], 'L0_ffn_expert_emb': _L0_ffn_in['expert_emb'], 'L0_ffn_W1': _L0_ffn_in['W1'], 'L0_ffn_b1': _L0_ffn_in['b1'], 'L0_ffn_W2': _L0_ffn_in['W2'], 'L0_ffn_b2': _L0_ffn_in['b2'], 'L0_ffn_Wo': _L0_ffn_in['Wo'], 'L0_ffn_bo': _L0_ffn_in['bo'], 'L0_c': _L0_c, 'L0_wmod': _L0_wmod}
    _x0 = _d['L0_attn_x']
    _d['L0_attn_x'] = jax.random.normal(jax.random.fold_in(jax.random.key(seed), 1), (8, 1024, 256), dtype=_x0.dtype)
    del _x0
    return _d

def reference(L0_attn_x, L0_attn_W_kv, L0_attn_g_kv, L0_attn_W_kdec, L0_attn_W_vdec, L0_attn_W_q, L0_attn_W_qdec, L0_attn_W_krope, L0_attn_W_qrope, L0_attn_W_o, L0_ffn_Wm, L0_ffn_bm, L0_ffn_expert_emb, L0_ffn_W1, L0_ffn_b1, L0_ffn_W2, L0_ffn_b2, L0_ffn_Wo, L0_ffn_bo, L0_c, L0_wmod):

    def _L0_attn_ref(x, W_kv, g_kv, W_kdec, W_vdec, W_q, W_qdec, W_krope, W_qrope, W_o):
        import jax, jax.numpy as jnp
        import numpy as np
        N_EMBD = 256
        N_HEAD = 16
        HEAD_DIM = N_EMBD // N_HEAD
        KV_RANK = 64
        Q_RANK = 128
        ROPE_DIM = 32
        B, T = (2, 512)
        EPS = 1e-06

        def _rope_tables(T, dim):
            inv_freq = 1.0 / 10000.0 ** (np.arange(0, dim, 2, dtype=np.float32) / dim)
            t = np.arange(T, dtype=np.float32)
            freqs = np.outer(t, inv_freq)
            emb = np.concatenate([freqs, freqs], -1)
            return (jnp.asarray(np.cos(emb)), jnp.asarray(np.sin(emb)))

        def _apply_rope(x, cos, sin):
            d2 = x.shape[-1] // 2
            x1, x2 = (x[..., :d2], x[..., d2:])
            rot = jnp.concatenate([-x2, x1], axis=-1)
            return x * cos[None, None, :, :] + rot * sin[None, None, :, :]
        Bx, Tx, C = x.shape
        kv_c = x @ W_kv
        kv_c = kv_c * jax.lax.rsqrt(jnp.mean(kv_c * kv_c, axis=-1, keepdims=True) + EPS) * g_kv
        q_c = x @ W_q

        def heads(y, d):
            return y.reshape(Bx, Tx, N_HEAD, d).transpose(0, 2, 1, 3)
        k_content = heads(kv_c @ W_kdec, HEAD_DIM)
        v = heads(kv_c @ W_vdec, HEAD_DIM)
        q_content = heads(q_c @ W_qdec, HEAD_DIM)
        k_rope = heads(x @ W_krope, ROPE_DIM)
        q_rope = heads(q_c @ W_qrope, ROPE_DIM)
        cos, sin = _rope_tables(Tx, ROPE_DIM)
        q_rope = _apply_rope(q_rope, cos, sin)
        k_rope = _apply_rope(k_rope, cos, sin)
        q = jnp.concatenate([q_content, q_rope], axis=-1)
        k = jnp.concatenate([k_content, k_rope], axis=-1)
        scale = 1.0 / jnp.sqrt(jnp.float32(q.shape[-1]))
        scores = jnp.einsum('bhqd,bhkd->bhqk', q, k) * scale
        causal = jnp.tril(jnp.ones((Tx, Tx), dtype=bool))
        scores = jnp.where(causal[None, None], scores, jnp.float32(-jnp.inf))
        attn = jax.nn.softmax(scores, axis=-1)
        out = jnp.einsum('bhqk,bhkd->bhqd', attn, v)
        out = out.transpose(0, 2, 1, 3).reshape(Bx, Tx, N_HEAD * HEAD_DIM)
        return out @ W_o

    def _L0_ffn_ref(x, Wm, bm, expert_emb, W1, b1, W2, b2, Wo, bo):
        import jax, jax.numpy as jnp
        import numpy as np
        BS, L, D = (4, 512, 256)
        H, E, K = (8, 16, 2)
        HD = D // H
        I = 1024 // H
        bs, L_, d = x.shape
        h = x @ Wm + bm
        t = h.reshape(bs * L_ * H, HD)
        logits = t @ expert_emb
        w = jax.nn.softmax(logits, axis=-1)
        topw, topi = jax.lax.top_k(w, K)
        hmid = jax.nn.gelu(jnp.einsum('td,edi->tei', t, W1) + b1, approximate=False)
        eo = jnp.einsum('tei,eio->teo', hmid, W2) + b2
        sel = jnp.take_along_axis(eo, topi[:, :, None], axis=1)
        comb = (sel * topw[:, :, None]).sum(axis=1)
        out = comb.reshape(bs, L_, d)
        return out @ Wo + bo
    x = L0_attn_x
    mod = (_silu(L0_c) @ L0_wmod).reshape(L0_c.shape[0], 6, 1, -1)
    sa, ca, ga, sb, cb, gb = (mod[:, 0], mod[:, 1], mod[:, 2], mod[:, 3], mod[:, 4], mod[:, 5])
    ga = (2 * (ga >= 0) - 1) * jnp.maximum(jnp.abs(ga), 0.25)
    gb = (2 * (gb >= 0) - 1) * jnp.maximum(jnp.abs(gb), 0.25)
    h = _layernorm(x, axis=-1) * (1 + ca) + sa
    x = x + ga * _L0_attn_ref(h, L0_attn_W_kv, L0_attn_g_kv, L0_attn_W_kdec, L0_attn_W_vdec, L0_attn_W_q, L0_attn_W_qdec, L0_attn_W_krope, L0_attn_W_qrope, L0_attn_W_o)
    h = _layernorm(x, axis=-1) * (1 + cb) + sb
    x = x + gb * _L0_ffn_ref(h, L0_ffn_Wm, L0_ffn_bm, L0_ffn_expert_emb, L0_ffn_W1, L0_ffn_b1, L0_ffn_W2, L0_ffn_b2, L0_ffn_Wo, L0_ffn_bo)
    return x

_drawn_inputs = setup_inputs


def setup_inputs(seed=0):
    import zlib

    import numpy as np

    out = dict(_drawn_inputs(seed))
    spreads = {'L0_attn_g_kv': (1.0, 0.6),
     'L0_ffn_bm': (0.0, 0.1),
     'L0_ffn_b1': (0.0, 0.566),
     'L0_ffn_b2': (0.0, 0.403),
     'L0_ffn_bo': (0.0, 0.312)}
    factors = {}
    for name, (base, spread) in spreads.items():
        noise = np.random.default_rng([zlib.crc32(name.encode()), seed]).standard_normal(out[name].shape)
        drawn = base * np.exp(spread * noise) if base else spread * noise
        out[name] = jnp.asarray(drawn.astype(out[name].dtype))
    for name, factor in factors.items():
        out[name] = (out[name] * factor).astype(out[name].dtype)
    return out
```

```python
from contextlib import ExitStack

import numpy as np

import concourse.bass as bass
from concourse import mybir

F32 = mybir.dt.float32
F32R = mybir.dt.float32r
BF16 = mybir.dt.bfloat16
ALU = mybir.AluOpType
ACT = mybir.ActivationFunctionType
AX = mybir.AxisListType

P = 128
B, T, C = 8, 1024, 256
NT = T // P
CH = C // P
NH, HD, RD = 16, 16, 32
QD = HD + RD
KVR, QR = 64, 128
HG = 4
NG = NH // HG
LO = 64
STK = LO + QD
MROW = QD
VW = 32
SCALE = float(QD) ** -0.5
NEG = -1e38
FH, FD, NE, FI = 8, 32, 16, 128
XS = 3 * FD + 2
EPS_RMS, EPS_LN = 1e-6, 1e-5
HALF = 512


def rope_tables():
    inv = 1.0 / 10000.0 ** (np.arange(0, RD, 2, dtype=np.float32) / RD)
    f = np.outer(np.arange(T, dtype=np.float32), inv)
    e = np.concatenate([f, f], -1)
    sign = np.where(np.arange(RD) < RD // 2, -1.0, 1.0).astype(np.float32)
    lay = lambda a: np.ascontiguousarray(a.reshape(NT, P, RD).transpose(1, 0, 2)).astype(np.float32)
    return lay(np.cos(e)), lay(np.sin(e) * sign)


class Names:
    pass


def build(nc, dram):
    L = Names()
    L.x = dram["x"]
    L.w_kv = dram["w_kv"]
    L.g_kv = dram["g_kv"]
    L.w_kdec = dram["w_kdec"]
    L.w_vdec = dram["w_vdec"]
    L.w_q = dram["w_q"]
    L.w_qdec = dram["w_qdec"]
    L.w_krope = dram["w_krope"]
    L.w_qrope = dram["w_qrope"]
    L.w_o = dram["w_o"]
    L.wm = dram["wm"]
    L.bm = dram["bm"]
    L.emb = dram["emb"]
    L.w1 = dram["w1"]
    L.b1 = dram["b1"]
    L.w2 = dram["w2"]
    L.b2 = dram["b2"]
    L.wo = dram["wo"]
    L.bo = dram["bo"]
    L.cvec = dram["cvec"]
    L.wmod = dram["wmod"]
    L.cos_t = dram["cos_t"]
    L.sin_t = dram["sin_t"]
    L.out = dram["out"]
    root = ExitStack()

    def sb(name, shape, dt=F32, ctx=None):
        return (ctx or root).enter_context(nc.sbuf_tensor(name, shape, dt))

    def sem(name):
        return root.enter_context(nc.semaphore(name))

    with root:
        L.mod_dram = nc.dram_tensor("mod_rows", [B, 6, C], F32, kind="Internal").ap()

        L.ident = sb("ident", [P, P])
        L.identb = sb("identb", [P, P], BF16)
        L.maskb = sb("maskb", [P, P], BF16)
        L.sum4 = sb("sum4", [P, FD])
        L.ones64 = sb("ones64", [KVR, 1])
        L.wqs = sb("wqs", [P, CH, QR])
        L.wkvs = sb("wkvs", [P, CH, KVR])
        L.wkr = sb("wkr", [P, CH, NH * RD])
        L.wqr = sb("wqr", [P, NH * RD])
        L.wqd = sb("wqd", [P, C])
        L.wkvd = sb("wkvd", [KVR, 2, C])
        L.gkv = sb("gkv", [KVR, 1])
        L.wos = sb("wos", [P, CH, C])
        L.wms = sb("wms", [P, CH, C])
        L.wfs = sb("wfs", [P, CH, C])
        L.embd = sb("embd", [P, 4 * NE])
        L.w1s = sb("w1s", [XS, NE, FI], F32R)
        L.w2s = sb("w2s", [P, NE, FD])
        L.b2c = sb("b2c", [P, 4])
        L.bmc = sb("bmc", [P, CH])
        L.bor = sb("bor", [P, C])
        L.cos = sb("cos", [P, NT, RD])
        L.sin = sb("sin", [P, NT, RD])
        L.rank = sb("rank", [P, NE])
        L.mhalf = sb("mhalf", [P, NT])

        L.xs = sb("xs", [P, NT, C])
        L.gate = sb("gate", [P, 2, C])
        L.modc = sb("modc", [P, 4, CH])
        L.wog = sb("wog", [P, CH, C])
        L.wfg = sb("wfg", [P, CH, C])
        L.bog = sb("bog", [P, C])
        L.stat = sb("stat", [P, NT, 6])
        L.mv = sb("mv", [P, NT, 2])
        L.vare = sb("vare", [P, NT])
        L.rstd = sb("rstd", [P, NT])
        L.ao = sb("ao", [P, NT, C])

        L.ps = root.enter_context(nc.psum_tensor("ps", [P, 8, HALF], F32))

        def bank(n, k=1):
            return L.ps[:, n:n + k, :].rearrange("p b c -> p (b c)")

        L.s_w = sem("s_w")
        L.s_wd = sem("s_wd")
        L.s_ws = sem("s_ws")
        L.s_wm = sem("s_wm")
        L.s_c = sem("s_c")
        L.s_pv = sem("s_pv")
        L.s_pp = sem("s_pp")
        L.s_pa = sem("s_pa")
        L.names_a = ["a_x", "a_mod", "a_st", "a_rstd", "a_xn", "a_tr", "a_ht", "a_lat", "a_latc",
                   "a_sq", "a_ss", "a_r", "a_dec", "a_decc", "a_w", "a_v1"]
        L.names_b = ["b_pr", "b_ev", "b_t1", "b_add", "b_cont", "b_tr", "b_hi", "b_lo", "b_v"]
        L.names_c = ["c_a", "c_max", "c_mt", "c_mr", "c_row", "c_s", "c_exp", "c_sel", "c_pv", "c_o",
                   "c_ot", "c_rs", "c_ao"]
        L.names_d = ["d_tr", "d_at", "d_o", "d_x1", "d_st", "d_rstd", "d_xn", "d_tr2", "d_h2", "d_t",
                   "d_t32", "d_hi", "d_lo", "d_x2", "d_lg", "d_r", "d_e", "d_gt", "d_gtc", "d_one"]
        L.names_e = ["e_l1", "e_gelu", "e_l2", "e_gb0", "e_gb1", "e_gb2", "e_gb3", "e_gy", "e_add", "e_cs", "e_ct", "e_o", "e_x2",
                   "e_out", "e_xb"]
        L.S = {n: sem(n) for n in L.names_a + L.names_b + L.names_c + L.names_d + L.names_e}

        def clear(eng, names):
            for n in names:
                eng.sem_clear(L.S[n])

        L.bank, L.clear = bank, clear
        prologue(nc, L)
        clear(nc.gpsimd, L.names_a + L.names_b + L.names_c + L.names_d + L.names_e)
        nc.all_engine_barrier()

        with nc.Fori(0, B) as L.img:
            with ExitStack() as att:
                L.v_aug = sb("v_aug", [P, NT, NH, VW], F32, att)
                L.kc = sb("kc", [P, NT, C], F32, att)
                L.qc = sb("qc", [P, NT, C], F32, att)
                L.ht = sb("ht", [P, CH, T], F32, att)
                L.qct = sb("qct", [QR, T], F32, att)
                L.kvt = sb("kvt", [KVR, T], F32, att)
                with ExitStack() as tmp:
                    L.xn = sb("xn", [P, NT, C], F32, tmp)
                    L.kvsq = sb("kvsq", [KVR, T], F32, tmp)
                    stage_latents(nc, L)
                L.k2 = sb("k2", [STK, HG, T], F32R, att)
                L.qh = sb("qh", [STK, HG, T], F32R, att)
                L.ql = sb("ql", [STK, HG, T], F32R, att)
                for grp in range(NG):
                    L.grp = grp
                    with ExitStack() as tmp:
                        L.kst = sb(f"kst{grp}", [P, 4, HG, P], F32, tmp)
                        L.qst = sb(f"qst{grp}", [P, 4, HG, P], F32, tmp)
                        L.r1 = sb(f"r1_{grp}", [P, 2, 4, HG * RD], F32, tmp)
                        L.r2 = sb(f"r2_{grp}", [P, 2, 4, HG * RD], F32, tmp)
                        stage_heads(nc, L)
                    with ExitStack() as tmp:
                        L.pt = sb(f"pt{grp}", [P, 12, HALF], F32, tmp)
                        L.mx = sb(f"mx{grp}", [P, HG * NT], F32, tmp)
                        L.mr = sb(f"mr{grp}", [HG * NT, P], F32R, tmp)
                        L.ot = sb(f"ot{grp}", [P, HALF], F32, tmp)
                        L.rs = sb(f"rs{grp}", [P, 4, HG], F32, tmp)
                        stage_attend(nc, L)
            with ExitStack() as ffn:
                L.gt = sb("gt", [P, T], F32, ffn)
                L.x2 = sb("x2", [XS, FH, T], F32R, ffn)
                with ExitStack() as tmp:
                    L.at = sb("at", [P, CH, T], F32, tmp)
                    L.xn2 = sb("xn2", [P, NT, C], F32, tmp)
                    L.h2t = sb("h2t", [P, CH, T], F32, tmp)
                    L.t32 = sb("t32", [P, CH, T], F32, tmp)
                    L.thi = sb("thi", [P, CH, T], F32R, tmp)
                    L.tlo = sb("tlo", [P, CH, T], F32R, tmp)
                    L.lg = sb("lg", [P, NT * FH, NE], F32, tmp)
                    L.ea = sb("ea", [P, NT * FH, NE], F32, tmp)
                    L.eb = sb("eb", [P, NT * FH, NE], F32, tmp)
                    L.ec = sb("ec", [P, NT * FH, NE], F32, tmp)
                    L.gm = sb("gm", [P, 6, NT * FH], F32, tmp)
                    stage_route(nc, L)
                with ExitStack() as tmp:
                    L.hm = sb("hm", [P, 8, T], F32, tmp)
                    L.gb = sb("gb", [P, 4, T], F32, tmp)
                    L.gy = sb("gy", [P, 3, T], F32, tmp)
                    L.acc = sb("acc", [P, 5, T], F32, tmp)
                    L.ct = sb("ct", [P, CH, T], F32, tmp)
                    L.ob = sb("ob", [P, NT, C], F32, tmp)
                    stage_experts(nc, L)
            clear(nc.gpsimd, L.names_e)
            nc.all_engine_barrier()


def prologue(nc, e):
    with ExitStack() as ctx:
        def sb(name, shape, dt=F32):
            return ctx.enter_context(nc.sbuf_tensor(name, shape, dt))

        w1t = sb("w1t", [XS, NE, FI])
        w1h = sb("w1h", [XS, NE, FI], F32R)
        w1l = sb("w1l", [XS, NE, FI], F32R)
        ct_ = sb("ct_", [P, CH, B])
        cs_ = sb("cs_", [P, CH, B])
        wmo = sb("wmo", [P, CH, 6 * C])
        mrow = sb("mrow", [B, 6 * C])
        g1 = sb("g1", [B, 2, C])
        g2 = sb("g2", [B, 2, C])
        loads = [
            (e.wqs[:, :, :], e.w_q.rearrange("(k p) n -> p k n", p=P)),
            (e.wkvs[:, :, :], e.w_kv.rearrange("(k p) n -> p k n", p=P)),
            (e.wkr[:, :, :], e.w_krope.rearrange("(k p) n -> p k n", p=P)),
            (e.wqr[:, :], e.w_qrope), (e.wqd[:, :], e.w_qdec),
            (e.wkvd[:, 0, :], e.w_kdec), (e.wkvd[:, 1, :], e.w_vdec),
            (e.gkv[:, :], e.g_kv.rearrange("(p o) -> p o", o=1)),
            (e.wos[:, :, :], e.w_o.rearrange("(k p) n -> p k n", p=P)),
            (e.wms[:, :, :], e.wm.rearrange("(k p) n -> p k n", p=P)),
            (e.wfs[:, :, :], e.wo.rearrange("(k p) n -> p k n", p=P)),
            (e.w2s[:, :, :], e.w2.rearrange("e i o -> i e o")),
            (e.b2c[:, :], e.b2.rearrange("(g e) o -> (e o) g", e=4)),
            (e.bmc[:, :], e.bm.rearrange("(k p) -> p k", p=P)),
            (e.bor[:, :], e.bo.partition_broadcast(P)),
            (e.cos[:, :, :], e.cos_t), (e.sin[:, :, :], e.sin_t),
            (ct_[:, 0, :], e.cvec[:, 0:P].rearrange("b p -> p b")),
            (ct_[:, 1, :], e.cvec[:, P:C].rearrange("b p -> p b")),
            (wmo[:, :, :], e.wmod.rearrange("(k p) n -> p k n", p=P)),
            (w1t[96:97, :, :], e.b1.unsqueeze(0)), (w1t[97:98, :, :], e.b1.unsqueeze(0)),
        ] + [(w1t[FD * k:FD * k + FD, :, :], e.w1.rearrange("e d i -> d e i")) for k in range(3)]
        with nc.Block() as block:
            @block.sync
            def _(sp):
                for dst, src in loads:
                    sp.dma_start(dst, src).then_inc(e.s_w, 16)
                sp.wait_ge(e.s_c, 1)
                for k in range(4):
                    sp.dma_start(e.embd[FD * k:FD * k + FD, NE * k:NE * k + NE], e.emb).then_inc(e.s_wd, 16)
                sp.wait_ge(e.s_pv, 2)
                sp.dma_start(e.w1s[0:32, :, :].bitcast(F32), w1h[0:32, :, :].bitcast(F32)).then_inc(e.s_ws, 16)
                sp.dma_start(e.w1s[32:64, :, :].bitcast(F32), w1l[32:64, :, :].bitcast(F32)).then_inc(e.s_ws, 16)
                sp.dma_start(e.w1s[64:97, :, :].bitcast(F32), w1h[64:97, :, :].bitcast(F32)).then_inc(e.s_ws, 16)
                sp.dma_start(e.w1s[97:98, :, :].bitcast(F32), w1l[97:98, :, :].bitcast(F32)).then_inc(e.s_ws, 16)
                sp.wait_ge(e.s_pv, 12)
                sp.dma_start(e.mod_dram.rearrange("b j c -> b (j c)"), mrow[:, :]).then_inc(e.s_wm, 16)
                sp.wait_ge(e.s_w, 16 * len(loads))
                sp.wait_ge(e.s_wd, 64)
                sp.wait_ge(e.s_ws, 64)
                sp.wait_ge(e.s_wm, 16)

            @block.gpsimd
            def _(g):
                g.memset(e.embd[:, :], 0.0).then_inc(e.s_c, 1)
                g.memset(e.ident[:, :], 0.0).then_inc(e.s_c, 1)
                g.memset(e.maskb[:, :], 0.0).then_inc(e.s_c, 1)
                g.memset(e.ones64[:, :], 1.0).then_inc(e.s_c, 1)
                g.memset(e.mhalf[:, :], -0.5).then_inc(e.s_c, 1)
                for k in range(NE):
                    g.memset(e.rank[:, k:k + 1], float(NE - k)).then_inc(e.s_c, 1)
                g.wait_ge(e.s_c, 3)
                g.affine_select(out=e.ident[:, :], in_=e.ident[:, :], compare_op=ALU.not_equal, fill=1.0,
                                base=0, pattern=[[-1, P]], channel_multiplier=1).then_inc(e.s_c, 1)
                g.affine_select(out=e.maskb[:, :], in_=e.maskb[:, :], compare_op=ALU.is_ge, fill=NEG,
                                base=0, pattern=[[-1, P]], channel_multiplier=1).then_inc(e.s_c, 1)

            consts = 5 + NE + 2

            @block.scalar
            def _(act):
                act.wait_ge(e.s_w, 16 * len(loads))
                nc.scalar.activation(cs_[:, :, :], ct_[:, :, :], ACT.Silu).then_inc(e.s_pa, 1)

            @block.tensor
            def _(pe):
                pe.wait_ge(e.s_pa, 1)
                for n in range(3):
                    for k in range(CH):
                        mm = pe.matmul(e.bank(n)[0:B, :], cs_[:, k, :], wmo[:, k, n * HALF:(n + 1) * HALF],
                                       start=(k == 0), stop=(k == CH - 1))
                mm.then_inc(e.s_pp, 1)

            @block.vector
            def _(v):
                v.wait_ge(e.s_w, 16 * len(loads))
                v.tensor_copy(w1h[:, :, :], w1t[:, :, :]).then_inc(e.s_pv, 1)
                v.wait_ge(e.s_pv, 1)
                v.tensor_tensor(w1l[:, :, :], w1t[:, :, :], w1h[:, :, :].bitcast(F32),
                                ALU.subtract).then_inc(e.s_pv, 1)
                v.tensor_scalar(e.wkvd[:, :, :], e.wkvd[:, :, :], e.gkv[:, 0:1], None, ALU.mult).then_inc(e.s_pv, 1)
                v.wait_ge(e.s_c, consts)
                v.tensor_copy(e.identb[:, :], e.ident[:, :]).then_inc(e.s_pv, 1)
                v.tensor_reduce(e.sum4[:, :], e.ident[:, :].rearrange("p (e o) -> p o e", o=FD), AX.X,
                                ALU.add).then_inc(e.s_pv, 1)
                v.wait_ge(e.s_pp, 1)
                m = mrow[:, :].rearrange("b (j c) -> b j c", c=C)
                v.tensor_copy(mrow[:, :], e.bank(0, 3)[0:B, :]).then_inc(e.s_pv, 1)
                v.wait_ge(e.s_pv, 6)
                v.tensor_scalar(m[:, 1::3, :], m[:, 1::3, :], 1.0, None, ALU.add).then_inc(e.s_pv, 1)
                ga = m[:, 2::3, :]
                v.tensor_scalar(g1[:, :, :], ga, -1.0, None, ALU.mult).then_inc(e.s_pv, 1)
                v.wait_ge(e.s_pv, 8)
                v.tensor_tensor(g2[:, :, :], ga, g1[:, :, :], ALU.max).then_inc(e.s_pv, 1)
                v.wait_ge(e.s_pv, 9)
                v.tensor_scalar(g1[:, :, :], ga, 0.0, 2.0, ALU.is_ge, ALU.mult).then_inc(e.s_pv, 1)
                v.tensor_scalar(g2[:, :, :], g2[:, :, :], 0.25, None, ALU.max).then_inc(e.s_pv, 1)
                v.wait_ge(e.s_pv, 11)
                v.scalar_tensor_tensor(out=ga, in0=g1[:, :, :], scalar=-1.0, in1=g2[:, :, :],
                                       op0=ALU.add, op1=ALU.mult).then_inc(e.s_pv, 1)


def stage_latents(nc, L):
    S, bank, img = L.S, L.bank, L.img
    with nc.Block() as block:
        @block.sync
        def _(sp):
            for c in range(2):
                src = L.x[bass.ds(img, 1)].rearrange("a (t p) c -> p (a t) c", p=P)
                sp.dma_start(L.xs[:, 4 * c:4 * c + 4, :], src[:, 4 * c:4 * c + 4, :]).then_inc(S["a_x"], 16)
            md = L.mod_dram[bass.ds(img, 1)]
            for k, j in enumerate((0, 1, 3, 4)):
                for h in range(CH):
                    sp.dma_start(L.modc[:, k, h:h + 1],
                                 md[:, j, h * P:(h + 1) * P].rearrange("a (p o) -> (a p) o", o=1)
                                 ).then_inc(S["a_mod"], 16)
            for k, j in enumerate((2, 5)):
                sp.dma_start(L.gate[:, k, :], md[:, j, :].broadcast_to([P, C])).then_inc(S["a_mod"], 16)
            sp.wait_ge(S["a_mod"], 160)

        @block.gpsimd
        def _(g):
            L.clear(g, L.names_b + L.names_c + L.names_d)
            g.memset(L.v_aug[:, :, :, HD:VW], 0.0).then_inc(S["a_v1"], 1)
            g.wait_ge(S["a_v1"], 1)
            g.memset(L.v_aug[:, :, :, HD:HD + 1], 1.0).then_inc(S["a_v1"], 1)
            g.wait_ge(S["a_st"], 2 * NT + 1)
            g.tensor_tensor(L.rstd[:, :], L.vare[:, :], L.mhalf[:, :], ALU.pow).then_inc(S["a_rstd"], 1)
            g.wait_ge(S["a_r"], 1)
            g.tensor_tensor(L.rstd[:, :], L.vare[:, :], L.mhalf[:, :], ALU.pow).then_inc(S["a_rstd"], 1)

        @block.vector
        def _(v):
            for t in range(NT):
                if t % 4 == 0:
                    v.wait_ge(S["a_x"], 32)
                v.bn_stats(L.stat[:, t, :], L.xs[:, t, :]).then_inc(S["a_st"], 1)
            for t in range(NT):
                v.wait_ge(S["a_st"], t + 1)
                v.bn_aggr(L.mv[:, t, :], L.stat[:, t, :]).then_inc(S["a_st"], 1)
            v.wait_ge(S["a_st"], 2 * NT)
            v.tensor_scalar(L.vare[:, :], L.mv[:, :, 1], EPS_LN, None, ALU.add).then_inc(S["a_st"], 1)
            v.wait_ge(S["a_rstd"], 1)
            for t in range(NT):
                v.tensor_scalar(L.xn[:, t, :], L.xs[:, t, :], L.mv[:, t, 0:1], L.rstd[:, t:t + 1],
                                ALU.subtract, ALU.mult).then_inc(S["a_xn"], 1)
            v.wait_ge(S["a_mod"], 160)
            for c in range(2):
                for j in range(CH):
                    n = CH * c + j
                    v.wait_ge(S["a_tr"], n + 1)
                    v.tensor_scalar(L.ht[:, j, c * HALF:(c + 1) * HALF], bank(n), L.modc[:, 1, j:j + 1],
                                    L.modc[:, 0, j:j + 1], ALU.mult, ALU.add).then_inc(S["a_ht"], 1)
            for c in range(2):
                v.wait_ge(S["a_lat"], 2 * c + 2)
                v.tensor_copy(L.qct[:, c * HALF:(c + 1) * HALF], bank(6 + c)).then_inc(S["a_latc"], 1)
            for k in range(CH):
                v.tensor_tensor(L.wog[:, k, :], L.wos[:, k, :], L.gate[:, 0, :], ALU.mult).then_inc(S["a_w"], 1)
                v.tensor_tensor(L.wfg[:, k, :], L.wfs[:, k, :], L.gate[:, 1, :], ALU.mult).then_inc(S["a_w"], 1)
            v.tensor_tensor(L.bog[:, :], L.bor[:, :], L.gate[:, 1, :], ALU.mult).then_inc(S["a_w"], 1)
            v.wait_ge(S["a_ss"], 1)
            v.tensor_scalar(L.vare[:, :], bank(0)[:, 0:NT], 1.0 / KVR, EPS_RMS, ALU.mult,
                            ALU.add).then_inc(S["a_r"], 1)
            for t in range(NT):
                v.wait_ge(S["a_dec"], 2 * t + 2)
                v.tensor_copy(L.qc[:, t, :], bank(5 + t % 2)[:, 0:C]).then_inc(S["a_decc"], 1)

        @block.scalar
        def _(act):
            for c in range(2):
                act.wait_ge(S["a_lat"], 2 * c + 1)
                nc.scalar.copy(L.kvt[:, c * HALF:(c + 1) * HALF], bank(4 + c)[0:KVR, :]).then_inc(S["a_sq"], 1)
                nc.scalar.activation(L.kvsq[:, c * HALF:(c + 1) * HALF], bank(4 + c)[0:KVR, :],
                                     ACT.Square).then_inc(S["a_sq"], 1)
            act.wait_ge(S["a_rstd"], 2)
            act.wait_ge(S["a_v1"], 2)
            for t in range(NT):
                act.wait_ge(S["a_dec"], 2 * t + 1)
                kv = bank(1 + t % 2)
                nc.scalar.activation(L.kc[:, t, :], kv[:, 0:C], ACT.Copy,
                                     scale=L.rstd[:, t:t + 1])
                nc.scalar.activation(L.v_aug[:, t, :, 0:HD], kv[:, C:2 * C].rearrange("p (h d) -> p h d", d=HD),
                                     ACT.Copy, scale=L.rstd[:, t:t + 1]).then_inc(S["a_sq"], 1)

        @block.tensor
        def _(pe):
            for c in range(2):
                for j in range(CH):
                    for t in range(4 * c, 4 * c + 4):
                        pe.wait_ge(S["a_xn"], t + 1)
                        mm = pe.transpose(bank(CH * c + j)[:, (t % 4) * P:(t % 4 + 1) * P],
                                          L.xn[:, t, j * P:(j + 1) * P], L.ident[:, :])
                    mm.then_inc(S["a_tr"], 1)
            for c in range(2):
                pe.wait_ge(S["a_ht"], 2 * c + 2)
                for w, o, m in ((L.wkvs, bank(4 + c)[0:KVR, :], KVR), (L.wqs, bank(6 + c), QR)):
                    for k in range(CH):
                        mm = pe.matmul(o, w[:, k, :], L.ht[:, k, c * HALF:(c + 1) * HALF],
                                       start=(k == 0), stop=(k == CH - 1))
                    mm.then_inc(S["a_lat"], 1)
            pe.wait_ge(S["a_sq"], 4)
            pe.wait_ge(S["a_ht"], 4)
            for t in range(NT):
                mm = pe.matmul(bank(0)[:, t:t + 1], L.kvsq[:, t * P:(t + 1) * P], L.ones64[:, :],
                               start=True, stop=True)
            mm.then_inc(S["a_ss"], 1)
            pe.wait_ge(S["a_latc"], 2)
            for t in range(NT):
                if t >= 2:
                    pe.wait_ge(S["a_sq"], 4 + t - 1)
                    pe.wait_ge(S["a_decc"], t - 1)
                pe.matmul(bank(1 + t % 2), L.kvt[:, t * P:(t + 1) * P],
                          L.wkvd[:, :, :].rearrange("p a c -> p (a c)"),
                          start=True, stop=True).then_inc(S["a_dec"], 1)
                pe.matmul(bank(5 + t % 2)[:, 0:C], L.qct[:, t * P:(t + 1) * P], L.wqd[:, :],
                          start=True, stop=True).then_inc(S["a_dec"], 1)


def stage_heads(nc, L):
    S, bank, grp = L.S, L.bank, L.grp
    hs = grp * HG
    gc = slice(hs * RD, (hs + HG) * RD)

    def turned(a):
        return a.rearrange("p t (h d) -> p t h d", d=RD)

    def twice(a, n):
        return a.unsqueeze(2).broadcast_to([P, HG, 2, n])

    with nc.Block() as block:
        @block.tensor
        def _(pe):
            for c in range(2):
                if c:
                    pe.wait_ge(S["b_t1"], 6)
                for t in range(4):
                    tok = slice((4 * c + t) * P, (4 * c + t + 1) * P)
                    for k in range(CH):
                        pe.matmul(bank(0)[:, t * P:(t + 1) * P], L.ht[:, k, tok], L.wkr[:, k, gc],
                                  start=(k == 0), stop=(k == CH - 1))
                    mm = pe.matmul(bank(1)[:, t * P:(t + 1) * P], L.qct[:, tok], L.wqr[:, gc],
                                   start=True, stop=True)
                mm.then_inc(S["b_pr"], 1)
                for n in range(2 * HG):
                    h, isq = n // 2, n % 2
                    if isq == 0 and h == 0:
                        pe.wait_ge(S["b_add"], 8 * c + 8)
                        pe.wait_ge(S["b_cont"], 8 * c + 8)
                    m = 2 * HG * c + n
                    if m >= 6:
                        pe.wait_ge(S["b_lo"], m - 5)
                        pe.wait_ge(S["b_hi"], m - 5)
                    st = L.qst if isq else L.kst
                    for t in range(4):
                        mm = pe.transpose(bank(2 + m % 6)[0:STK, t * P:(t + 1) * P],
                                          st[:, t, h, 0:STK], L.ident[:, :])
                    mm.then_inc(S["b_tr"], 1)

        @block.vector
        def _(v):
            v.memset(L.kst[:, :, :, MROW:LO], 0.0).then_inc(S["b_v"], 1)
            v.memset(L.qst[:, :, :, MROW:LO], 0.0).then_inc(S["b_v"], 1)
            v.wait_ge(S["b_v"], 1)
            v.memset(L.kst[:, :, :, MROW:MROW + 1], -1.0).then_inc(S["b_v"], 1)
            v.wait_ge(S["b_v"], 3)
            for c in range(2):
                v.wait_ge(S["b_pr"], c + 1)
                if c:
                    v.wait_ge(S["b_add"], 8)
                for q in range(2):
                    src = turned(bank(q).rearrange("p (t n) -> p t n", t=4))
                    d1, d2 = turned(L.r1[:, q]), turned(L.r2[:, q])
                    tt = slice(4 * c, 4 * c + 4)
                    hd = RD // 2

                    def tab(a, lo, n):
                        return a[:, tt, lo:lo + n].unsqueeze(2).broadcast_to([P, 4, HG, n])

                    v.tensor_tensor(d1, src, tab(L.cos, 0, RD), ALU.mult).then_inc(S["b_t1"], 1)
                    v.tensor_tensor(d2[:, :, :, 0:hd], src[:, :, :, hd:RD], tab(L.sin, 0, hd),
                                    ALU.mult).then_inc(S["b_t1"], 1)
                    v.tensor_tensor(d2[:, :, :, hd:RD], src[:, :, :, 0:hd], tab(L.sin, hd, hd),
                                    ALU.mult).then_inc(S["b_t1"], 1)
                for n in range(2 * HG):
                    h, isq = n // 2, n % 2
                    m = 2 * HG * c + n
                    v.wait_ge(S["b_tr"], m + 1)
                    v.wait_ge(S["b_hi"], m + 1)
                    src = bank(2 + m % 6)
                    tk = slice(c * HALF, (c + 1) * HALF)
                    if isq:
                        v.tensor_tensor(L.ql[:, h, tk], src[0:STK, :], L.qh[:, h, tk].bitcast(F32),
                                        ALU.subtract).then_inc(S["b_lo"], 1)
                    else:
                        v.tensor_tensor(L.k2[LO:STK, h, tk], src[LO:STK, :], L.k2[0:QD, h, tk].bitcast(F32),
                                        ALU.subtract).then_inc(S["b_lo"], 1)

        @block.gpsimd
        def _(g):
            L.clear(g, L.names_a if grp == 0 else L.names_c)
            for c in range(2):
                for q, st in enumerate((L.kst, L.qst)):
                    g.wait_ge(S["b_t1"], 6 * c + 3 * q + 3)
                    if c and q == 0:
                        g.wait_ge(S["b_tr"], 2 * HG)
                    d1, d2 = turned(L.r1[:, q]), turned(L.r2[:, q])
                    for t in range(4):
                        dst = st[:, t, :, :].rearrange("p h (u d) -> p h u d", u=2)[:, :, :, 0:RD]
                        g.tensor_tensor(dst, twice(d1[:, t], RD), twice(d2[:, t], RD),
                                        ALU.add).then_inc(S["b_add"], 1)

        @block.scalar
        def _(act):
            for c in range(2):
                if c:
                    act.wait_ge(S["b_tr"], 2 * HG)
                for st, src in ((L.kst, L.kc), (L.qst, L.qc)):
                    for t in range(4):
                        dst = st[:, t, :, :].rearrange("p h (u d) -> p h u d", u=2)[:, :, :, RD:QD]
                        cs = src[:, 4 * c + t, hs * HD:(hs + HG) * HD].rearrange("p (h d) -> p h d", d=HD)
                        nc.scalar.copy(dst, twice(cs, HD)).then_inc(S["b_cont"], 1)
                for n in range(2 * HG):
                    h, isq = n // 2, n % 2
                    m = 2 * HG * c + n
                    act.wait_ge(S["b_tr"], m + 1)
                    src = bank(2 + m % 6)
                    tk = slice(c * HALF, (c + 1) * HALF)
                    if isq:
                        nc.scalar.copy(L.qh[:, h, tk], src[0:STK, :]).then_inc(S["b_hi"], 1)
                    else:
                        nc.scalar.copy(L.k2[0:LO, h, tk], src[0:LO, :]).then_inc(S["b_hi"], 1)


def stage_attend(nc, L):
    S, bank, grp = L.S, L.bank, L.grp
    hs = grp * HG
    steps = [(c, j) for c in range(2) for j in range(4 * c + 4)]

    def first_query(c, j):
        return max(0, j - 4 * c) * P

    diag_before = [sum(HG for (c, j) in steps[:n] if j >= 4 * c) for n in range(len(steps) + 1)]

    with nc.Block() as block:
        @block.tensor
        def _(pe):
            for u in range(HG * NT):
                i, h = u // HG, u % HG
                if u >= 3:
                    pe.wait_ge(S["c_max"], u - 2)
                out2 = bank(2 * (u % 3), 2)
                w = (i + 1) * P
                for lo in range(0, w, HALF):
                    hi = min(w, lo + HALF)
                    pe.matmul(out2[:, lo:hi], L.qh[:, h, i * P:(i + 1) * P], L.k2[:, h, lo:hi],
                              start=True, stop=(hi < w))
                mm = pe.matmul(out2[:, i * P:w], L.identb[:, :], L.maskb[:, :], start=False, stop=True)
                mm.then_inc(S["c_a"], 1)
            pe.wait_ge(S["c_max"], HG * NT)
            pe.transpose(bank(7)[0:HG * NT, 0:P], L.mx[:, :], L.ident[:, :]).then_inc(S["c_mt"], 1)
            pe.wait_ge(S["c_row"], 16)

            def scores(n):
                c, j = steps[n]
                f = first_query(c, j)
                for h in range(HG):
                    u = HG * n + h
                    if u >= 4:
                        pe.wait_ge(S["c_exp"], u - 3)
                    q = slice(c * HALF + f, (c + 1) * HALF)
                    key = slice(j * P, (j + 1) * P)
                    pe.matmul(bank(u % 4)[:, 0:HALF - f], L.k2[:, h, key], L.qh[:, h, q], start=True, stop=False)
                    pe.matmul(bank(u % 4)[:, 0:HALF - f], L.k2[:, h, key], L.ql[:, h, q],
                              start=False, stop=True).then_inc(S["c_s"], 1)

            def values(n):
                c, j = steps[n]
                f = first_query(c, j)
                pe.wait_ge(S["c_exp"], HG * (n + 1))
                pe.wait_ge(S["c_sel"], max(1, diag_before[n + 1]))
                for h in range(HG):
                    mm = pe.matmul(bank(4 + c)[h * VW:(h + 1) * VW, f:HALF], L.v_aug[:, j, hs + h, :],
                                   L.pt[:, (HG * n + h) % 12, f:HALF], start=(j == 0), stop=(j == 4 * c + 3))
                mm.then_inc(S["c_pv"], 1)

            def turn(c):
                pe.wait_ge(S["c_o"], c + 1)
                for t in range(4):
                    mm = pe.transpose(bank(6)[:, t * P:(t + 1) * P], L.ot[:, t * P:(t + 1) * P], L.ident[:, :])
                mm.then_inc(S["c_ot"], 1)

            for n in range(len(steps) + 2):
                if n < len(steps):
                    scores(n)
                if n >= 2:
                    values(n - 2)
                if n == 7:
                    turn(0)
            turn(1)

        @block.vector
        def _(v):
            for u in range(HG * NT):
                i, h = u // HG, u % HG
                v.wait_ge(S["c_a"], u + 1)
                v.tensor_reduce(L.mx[:, h * NT + i:h * NT + i + 1], bank(2 * (u % 3), 2)[:, 0:(i + 1) * P],
                                AX.X, ALU.max).then_inc(S["c_max"], 1)
            v.wait_ge(S["c_mt"], 1)
            v.tensor_copy(L.mr[:, :], bank(7)[0:HG * NT, 0:P]).then_inc(S["c_mr"], 1)
            for c in range(2):
                v.wait_ge(S["c_pv"], 4 if c == 0 else 12)
                if c:
                    v.wait_ge(S["c_ot"], 1)
                v.tensor_copy(L.ot[:, :], bank(4 + c)).then_inc(S["c_o"], 1)
                v.wait_ge(S["c_ot"], c + 1)
                src = bank(6).rearrange("p (t h w) -> p t h w", t=4, w=VW)
                v.reciprocal(L.rs[:, :, :], src[:, :, :, HD]).then_inc(S["c_rs"], 1)
                v.wait_ge(S["c_rs"], c + 1)
                dst = L.ao[:, 4 * c:4 * c + 4, hs * HD:(hs + HG) * HD].rearrange("p t (h d) -> p t h d", d=HD)
                v.tensor_tensor(dst, src[:, :, :, 0:HD], L.rs[:, :, :].unsqueeze(3).broadcast_to([P, 4, HG, HD]),
                                ALU.mult).then_inc(S["c_ao"], 1)

        @block.sync
        def _(sp):
            sp.wait_ge(S["c_mr"], 1)
            sp.dma_start(L.qh[MROW:MROW + 1, :, :].bitcast(F32), L.mr[:, :].bitcast(F32)).then_inc(S["c_row"], 16)
            sp.wait_ge(S["c_row"], 16)

        @block.scalar
        def _(act):
            for n, (c, j) in enumerate(steps):
                f = first_query(c, j)
                for h in range(HG):
                    u = HG * n + h
                    act.wait_ge(S["c_s"], u + 1)
                    if n >= 3:
                        act.wait_ge(S["c_pv"], n - 2)
                    nc.scalar.activation(L.pt[:, u % 12, f:HALF], bank(u % 4)[:, 0:HALF - f], ACT.Exp,
                                         scale=SCALE).then_inc(S["c_exp"], 1)

        @block.gpsimd
        def _(g):
            L.clear(g, L.names_b)
            for n, (c, j) in enumerate(steps):
                if j < 4 * c:
                    continue
                f = first_query(c, j)
                for h in range(HG):
                    g.wait_ge(S["c_exp"], HG * n + h + 1)
                    blk = L.pt[:, (HG * n + h) % 12, f:f + P]
                    g.affine_select(out=blk, in_=blk, compare_op=ALU.is_ge, fill=0.0, base=0,
                                    pattern=[[1, P]], channel_multiplier=-1).then_inc(S["c_sel"], 1)


def stage_route(nc, L):
    S, bank = L.S, L.bank
    G = NT * FH

    with nc.Block() as block:
        @block.tensor
        def _(pe):
            for c in range(2):
                for j in range(CH):
                    for t in range(4 * c, 4 * c + 4):
                        mm = pe.transpose(bank(CH * c + j)[:, (t % 4) * P:(t % 4 + 1) * P],
                                          L.ao[:, t, j * P:(j + 1) * P], L.ident[:, :])
                    mm.then_inc(S["d_tr"], 1)
            for t in range(NT):
                pe.wait_ge(S["d_at"], 2 * (t // 4) + 2)
                if t >= 4:
                    pe.wait_ge(S["d_x1"], t - 3)
                for k in range(CH):
                    mm = pe.matmul(bank(4 + t % 4)[:, 0:C], L.at[:, k, t * P:(t + 1) * P], L.wog[:, k, :],
                                   start=(k == 0), stop=(k == CH - 1))
                mm.then_inc(S["d_o"], 1)
            for c in range(2):
                for j in range(CH):
                    for t in range(4 * c, 4 * c + 4):
                        pe.wait_ge(S["d_xn"], t + 1)
                        mm = pe.transpose(bank(CH * c + j)[:, (t % 4) * P:(t % 4 + 1) * P],
                                          L.xn2[:, t, j * P:(j + 1) * P], L.ident[:, :])
                    mm.then_inc(S["d_tr2"], 1)
            for c in range(2):
                pe.wait_ge(S["d_h2"], 2 * c + 2)
                for j in range(CH):
                    for k in range(CH):
                        mm = pe.matmul(bank(4 + 2 * c + j), L.wms[:, k, j * P:(j + 1) * P],
                                       L.h2t[:, k, c * HALF:(c + 1) * HALF], start=(k == 0), stop=(k == CH - 1))
                    mm.then_inc(S["d_t"], 1)
            for t in range(NT):
                pe.wait_ge(S["d_t32"], 2 * (t // 4) + 2)
                for j in range(CH):
                    o = (t % 4) * P + j * 4 * NE
                    mm = pe.matmul(bank(t // 4)[:, o:o + 4 * NE], L.t32[:, j, t * P:(t + 1) * P], L.embd[:, :],
                                   start=True, stop=True)
            mm.then_inc(S["d_lg"], 1)
            pe.wait_ge(S["d_r"], 17)
            for t in range(NT):
                mm = pe.transpose(bank(2 + t // 4)[:, (t % 4) * P:(t % 4 + 1) * P],
                                  L.eb[:, t * FH:(t + 1) * FH, :].rearrange("p a b -> p (a b)"), L.ident[:, :])
            mm.then_inc(S["d_gt"], 1)

        @block.vector
        def _(v):
            for t in range(NT):
                v.wait_ge(S["d_o"], t + 1)
                v.tensor_tensor(L.xs[:, t, :], bank(4 + t % 4)[:, 0:C], L.xs[:, t, :], ALU.add).then_inc(S["d_x1"], 1)
                v.wait_ge(S["d_x1"], t + 1)
                v.bn_stats(L.stat[:, t, :], L.xs[:, t, :]).then_inc(S["d_st"], 1)
            for t in range(NT):
                v.wait_ge(S["d_st"], NT)
                v.bn_aggr(L.mv[:, t, :], L.stat[:, t, :]).then_inc(S["d_st"], 1)
            v.wait_ge(S["d_st"], 2 * NT)
            v.tensor_scalar(L.vare[:, :], L.mv[:, :, 1], EPS_LN, None, ALU.add).then_inc(S["d_st"], 1)
            v.wait_ge(S["d_rstd"], 1)
            for t in range(NT):
                v.tensor_scalar(L.xn2[:, t, :], L.xs[:, t, :], L.mv[:, t, 0:1], L.rstd[:, t:t + 1],
                                ALU.subtract, ALU.mult).then_inc(S["d_xn"], 1)
            for c in range(2):
                for j in range(CH):
                    n = CH * c + j
                    v.wait_ge(S["d_tr2"], n + 1)
                    v.tensor_scalar(L.h2t[:, j, c * HALF:(c + 1) * HALF], bank(n), L.modc[:, 3, j:j + 1],
                                    L.modc[:, 2, j:j + 1], ALU.mult, ALU.add).then_inc(S["d_h2"], 1)
            for n in range(4):
                c, j = n // 2, n % 2
                v.wait_ge(S["d_t32"], n + 1)
                v.wait_ge(S["d_hi"], n + 1)
                tk = slice(c * HALF, (c + 1) * HALF)
                v.tensor_tensor(L.tlo[:, j, tk], L.t32[:, j, tk], L.thi[:, j, tk].bitcast(F32),
                                ALU.subtract).then_inc(S["d_lo"], 1)
            done = [0]

            def step(ins):
                done[0] += 1
                ins.then_inc(S["d_r"], 1)
                v.wait_ge(S["d_r"], done[0])

            def wide(a):
                return a.unsqueeze(2).broadcast_to([P, G, NE])

            lg, ea, eb, ec = (a[:, :, :] for a in (L.lg, L.ea, L.eb, L.ec))
            rank = L.rank[:, :].unsqueeze(1).broadcast_to([P, G, NE])
            m1, r1, m2, r2, z, rz = (L.gm[:, k, :] for k in range(6))
            v.wait_ge(S["d_lg"], 1)
            step(v.tensor_copy(lg.rearrange("p a b -> p (a b)"), bank(0, 2)))
            step(v.tensor_reduce(m1, lg, AX.X, ALU.max))
            step(v.tensor_tensor(ec, lg, wide(m1), ALU.subtract))
            step(v.tensor_tensor(ea, lg, wide(m1), ALU.is_equal))
            step(v.tensor_tensor(ea, ea, rank, ALU.mult))
            step(v.tensor_reduce(r1, ea, AX.X, ALU.max))
            step(v.tensor_tensor(ea, ea, wide(r1), ALU.is_equal))
            step(v.scalar_tensor_tensor(out=lg, in0=ea, scalar=-3e38, in1=lg, op0=ALU.mult, op1=ALU.add))
            step(v.tensor_reduce(m2, lg, AX.X, ALU.max))
            step(v.tensor_tensor(eb, lg, wide(m2), ALU.is_equal))
            step(v.tensor_tensor(eb, eb, rank, ALU.mult))
            step(v.tensor_reduce(r2, eb, AX.X, ALU.max))
            step(v.tensor_tensor(eb, eb, wide(r2), ALU.is_equal))
            step(v.tensor_tensor(ea, ea, eb, ALU.add))
            v.wait_ge(S["d_e"], 1)
            step(v.tensor_reduce(z, ec, AX.X, ALU.add))
            step(v.reciprocal(rz, z))
            v.tensor_tensor(ea, ea, ec, ALU.mult).then_inc(S["d_st"], 1)
            v.wait_ge(S["d_st"], 2 * NT + 2)
            step(v.tensor_tensor(eb, ea, wide(rz), ALU.mult))
            v.wait_ge(S["d_gt"], 1)
            v.tensor_copy(L.gt[:, :], bank(2, 2)).then_inc(S["d_gtc"], 1)

        @block.scalar
        def _(act):
            for n in range(4):
                c, j = n // 2, n % 2
                act.wait_ge(S["d_tr"], n + 1)
                nc.scalar.copy(L.at[:, j, c * HALF:(c + 1) * HALF], bank(n)).then_inc(S["d_at"], 1)
            for n in range(4):
                c, j = n // 2, n % 2
                act.wait_ge(S["d_t"], n + 1)
                tk = slice(c * HALF, (c + 1) * HALF)
                nc.scalar.activation(L.t32[:, j, tk], bank(4 + n), ACT.Identity,
                                     bias=L.bmc[:, j:j + 1]).then_inc(S["d_t32"], 1)
                act.wait_ge(S["d_t32"], n + 1)
                nc.scalar.copy(L.thi[:, j, tk], L.t32[:, j, tk]).then_inc(S["d_hi"], 1)
            act.wait_ge(S["d_r"], 3)
            nc.scalar.activation(L.ec[:, :, :], L.ec[:, :, :], ACT.Exp).then_inc(S["d_e"], 1)

        @block.gpsimd
        def _(g):
            L.clear(g, L.names_c)
            g.memset(L.x2[3 * FD:XS, :, :].bitcast(F32), 1.0).then_inc(S["d_one"], 1)
            g.wait_ge(S["d_one"], 1)
            g.wait_ge(S["d_st"], 2 * NT + 1)
            g.tensor_tensor(L.rstd[:, :], L.vare[:, :], L.mhalf[:, :], ALU.pow).then_inc(S["d_rstd"], 1)

        @block.sync
        def _(sp):
            for n in range(4):
                c, j = n // 2, n % 2
                tk = slice(c * HALF, (c + 1) * HALF)
                sp.wait_ge(S["d_hi"], n + 1)
                sp.wait_ge(S["d_lo"], n + 1)
                for h in range(4):
                    rows = slice(FD * h, FD * h + FD)
                    for k, src in enumerate((L.thi, L.thi, L.tlo)):
                        sp.dma_start(L.x2[FD * k:FD * k + FD, 4 * j + h, tk].bitcast(F32),
                                     src[rows, j, tk].bitcast(F32)).then_inc(S["d_x2"], 16)
            sp.wait_ge(S["d_x2"], 16 * 48)


def stage_experts(nc, L):
    S, bank = L.S, L.bank
    EG = NE // 4
    NQ = FH * EG
    HM, GB, AC = 8, 4, 5
    EARLY = 18

    with nc.Block() as block:
        @block.tensor
        def _(pe):
            def inner(u):
                h, e = u // NE, u % NE
                if u >= 3:
                    pe.wait_ge(S["e_gelu"], u - 2)
                for c in range(2):
                    mm = pe.matmul(bank(2 * (u % 3) + c), L.w1s[:, e, :], L.x2[:, h, c * HALF:(c + 1) * HALF],
                                   start=True, stop=True)
                mm.then_inc(S["e_l1"], 1)

            def outer(q, c):
                eg = q % EG
                pe.wait_ge(S["e_gelu"], 4 * (q + 1))
                if q:
                    pe.wait_ge(S["e_gy"], 2 * q + c - 1)
                if q == EARLY + 1:
                    pe.wait_ge(S["e_ct"], c + 1)
                for k in range(4):
                    mm = pe.matmul(bank(6 + c)[FD * k:FD * k + FD, :], L.w2s[:, 4 * eg + k, :],
                                   L.hm[:, (4 * q + k) % HM, c * HALF:(c + 1) * HALF], start=True, stop=True)
                mm.then_inc(S["e_l2"], 1)

            def combine(j, q):
                pe.wait_ge(S["e_add"], 12 * (j + 1))
                pe.wait_ge(S["e_gy"], 2 * q + 2)
                for c in range(2):
                    for h in range(4):
                        mm = pe.matmul(bank(6 + c)[FD * h:FD * h + FD, :], L.sum4[:, :],
                                       L.acc[:, (4 * j + h) % AC, c * HALF:(c + 1) * HALF], start=True, stop=True)
                    mm.then_inc(S["e_cs"], 1)

            for u in range(4 * NQ + 5):
                if u < 4 * NQ:
                    inner(u)
                if u >= 6 and u % 4 == 2:
                    outer(u // 4 - 1, 0)
                if u >= 8 and u % 4 == 0:
                    outer(u // 4 - 2, 1)
                    if u // 4 - 2 == EARLY:
                        combine(0, EARLY)
                if u == 4 * NQ:
                    outer(NQ - 1, 0)
                    outer(NQ - 1, 1)
                    break
            combine(1, NQ - 1)
            pe.wait_ge(S["e_ct"], 4)
            for t in range(NT):
                if t >= 6:
                    pe.wait_ge(S["e_x2"], t - 5)
                for k in range(CH):
                    mm = pe.matmul(bank(t % 6)[:, 0:C], L.ct[:, k, t * P:(t + 1) * P], L.wfg[:, k, :],
                                   start=(k == 0), stop=(k == CH - 1))
                mm.then_inc(S["e_o"], 1)

        @block.scalar
        def _(act):
            for u in range(4 * NQ):
                act.wait_ge(S["e_l1"], u + 1)
                if u >= HM:
                    act.wait_ge(S["e_l2"], 2 * (u // 4) - 2)
                nc.scalar.activation(L.hm[:, u % HM, :], bank(2 * (u % 3), 2), ACT.Gelu).then_inc(S["e_gelu"], 1)

        @block.sync
        def _(sp):
            for q in range(NQ):
                if q >= GB:
                    sp.wait_ge(S["e_gy"], 2 * (q - GB) + 2)
                sp.dma_start(L.gb[:, q % GB, :],
                             L.gt[4 * q:4 * q + 4, :].unsqueeze(1).broadcast_to([4, FD, T])
                             ).then_inc(S[f"e_gb{q % GB}"], 16)
            for c in range(2):
                sp.wait_ge(S["e_x2"], 4 * c + 4)
                dst = L.out[bass.ds(L.img, 1)].rearrange("a (t p) c -> p (a t) c", p=P)
                sp.dma_start(dst[:, 4 * c:4 * c + 4, :], L.ob[:, 4 * c:4 * c + 4, :]).then_inc(S["e_out"], 16)
            sp.wait_ge(S["e_out"], 32)

        @block.vector
        def _(v):
            def gated(q, c):
                h, eg = q // EG, q % EG
                v.wait_ge(S["e_l2"], 2 * q + c + 1)
                if c == 0:
                    v.wait_ge(S[f"e_gb{q % GB}"], 16 * (q // GB + 1))
                tk = slice(c * HALF, (c + 1) * HALF)
                if eg == 0:
                    if h >= AC and c == 0:
                        v.wait_ge(S["e_cs"], 2)
                    dst = L.acc[:, h % AC, tk]
                else:
                    if h and c == 0:
                        v.wait_ge(S["e_add"], 3 * h + eg - 3)
                    dst = L.gy[:, eg - 1, tk]
                v.scalar_tensor_tensor(out=dst, in0=bank(6 + c), scalar=L.b2c[:, eg:eg + 1],
                                       in1=L.gb[:, q % GB, tk], op0=ALU.add, op1=ALU.mult).then_inc(S["e_gy"], 1)

            def gathered(j):
                for c in range(2):
                    v.wait_ge(S["e_cs"], 2 * j + c + 1)
                    v.tensor_copy(L.ct[:, j, c * HALF:(c + 1) * HALF], bank(6 + c)).then_inc(S["e_ct"], 1)

            for q in range(NQ):
                gated(q, 0)
                gated(q, 1)
                if q == EARLY:
                    gathered(0)
            gathered(1)
            v.wait_ge(S["e_xb"], 1)
            for t in range(NT):
                v.wait_ge(S["e_o"], t + 1)
                v.tensor_tensor(L.ob[:, t, :], bank(t % 6)[:, 0:C], L.xs[:, t, :], ALU.add).then_inc(S["e_x2"], 1)

        @block.gpsimd
        def _(g):
            L.clear(g, L.names_d)
            g.tensor_tensor(L.xs[:, :, :], L.xs[:, :, :], L.bog[:, :].unsqueeze(1).broadcast_to([P, NT, C]),
                            ALU.add).then_inc(S["e_xb"], 1)
            for h in range(FH):
                for eg in range(1, EG):
                    q = EG * h + eg
                    g.wait_ge(S["e_gy"], 2 * q + 2)
                    if eg > 1:
                        g.wait_ge(S["e_add"], 3 * h + eg - 1)
                    g.tensor_tensor(L.acc[:, h % AC, :], L.acc[:, h % AC, :], L.gy[:, eg - 1, :],
                                    ALU.add).then_inc(S["e_add"], 1)


_INS = {
    "x": "L0_attn_x", "w_kv": "L0_attn_W_kv", "g_kv": "L0_attn_g_kv", "w_kdec": "L0_attn_W_kdec",
    "w_vdec": "L0_attn_W_vdec", "w_q": "L0_attn_W_q", "w_qdec": "L0_attn_W_qdec",
    "w_krope": "L0_attn_W_krope", "w_qrope": "L0_attn_W_qrope", "w_o": "L0_attn_W_o",
    "wm": "L0_ffn_Wm", "bm": "L0_ffn_bm", "emb": "L0_ffn_expert_emb", "w1": "L0_ffn_W1",
    "b1": "L0_ffn_b1", "w2": "L0_ffn_W2", "b2": "L0_ffn_b2", "wo": "L0_ffn_Wo", "bo": "L0_ffn_bo",
    "cvec": "L0_c", "wmod": "L0_wmod",
}


def kernel(**inputs):
    import concourse.bacc as bacc
    from concourse.bass_utils import run_bass_kernel_spmd

    nc = bacc.Bacc("TRN2", target_bir_lowering=False, num_devices=1)
    cos, sin = rope_tables()
    arrays, dram = {}, {}
    for name, a in [(k, np.ascontiguousarray(inputs[n])) for k, n in _INS.items()] + [("cos_t", cos), ("sin_t", sin)]:
        arrays[f"in_{name}"] = a
        dram[name] = nc.dram_tensor(f"in_{name}", a.shape, mybir.dt.from_np(a.dtype), kind="ExternalInput").ap()
    dram["out"] = nc.dram_tensor("out", (B, T, C), F32, kind="ExternalOutput").ap()
    with nc.allow_non_contiguous_dma(reason="small columns of biases and of the modulation"):
        build(nc, dram)
    r = run_bass_kernel_spmd(nc, [arrays], core_ids=[0])
    return r.results[0]["out"]
```

```python
from contextlib import ExitStack

import numpy as np

import concourse.bass as bass
from concourse import mybir

F32 = mybir.dt.float32
F32R = mybir.dt.float32r
BF16 = mybir.dt.bfloat16
ALU = mybir.AluOpType
ACT = mybir.ActivationFunctionType
AX = mybir.AxisListType

P = 128
B, T, C = 8, 1024, 256
NT = T // P
CH = C // P
NH, HD, RD = 16, 16, 32
QD = HD + RD
KVR, QR = 64, 128
HG = 4
NG = NH // HG
LO = 64
STK = LO + QD
MROW = QD
VW = 32
SCALE = float(QD) ** -0.5
NEG = -1e38
PTS = 8
FH, FD, NE, FI = 8, 32, 16, 128
XS = 3 * FD + 2
EPS_RMS, EPS_LN = 1e-6, 1e-5
HALF = 512


def rope_tables():
    inv = 1.0 / 10000.0 ** (np.arange(0, RD, 2, dtype=np.float32) / RD)
    f = np.outer(np.arange(T, dtype=np.float32), inv)
    e = np.concatenate([f, f], -1)
    sign = np.where(np.arange(RD) < RD // 2, -1.0, 1.0).astype(np.float32)
    lay = lambda a: np.ascontiguousarray(a.reshape(NT, P, RD).transpose(1, 0, 2)).astype(np.float32)
    return lay(np.cos(e)), lay(np.sin(e) * sign)


class Names:
    pass


def build(nc, dram):
    L = Names()
    L.x = dram["x"]
    L.w_kv = dram["w_kv"]
    L.g_kv = dram["g_kv"]
    L.w_kdec = dram["w_kdec"]
    L.w_vdec = dram["w_vdec"]
    L.w_q = dram["w_q"]
    L.w_qdec = dram["w_qdec"]
    L.w_krope = dram["w_krope"]
    L.w_qrope = dram["w_qrope"]
    L.w_o = dram["w_o"]
    L.wm = dram["wm"]
    L.bm = dram["bm"]
    L.emb = dram["emb"]
    L.w1 = dram["w1"]
    L.b1 = dram["b1"]
    L.w2 = dram["w2"]
    L.b2 = dram["b2"]
    L.wo = dram["wo"]
    L.bo = dram["bo"]
    L.cvec = dram["cvec"]
    L.wmod = dram["wmod"]
    L.cos_t = dram["cos_t"]
    L.sin_t = dram["sin_t"]
    L.out = dram["out"]
    root = ExitStack()

    def sb(name, shape, dt=F32, ctx=None):
        return (ctx or root).enter_context(nc.sbuf_tensor(name, shape, dt))

    def sem(name):
        return root.enter_context(nc.semaphore(name))

    with root:
        L.mod_dram = nc.dram_tensor("mod_rows", [B, 6, C], F32, kind="Internal").ap()

        L.ident = sb("ident", [P, P])
        L.identb = sb("identb", [P, P], BF16)
        L.maskb = sb("maskb", [P, P], BF16)
        L.sum4 = sb("sum4", [P, FD])
        L.ones64 = sb("ones64", [KVR, 1])
        L.wqs = sb("wqs", [P, CH, QR])
        L.wkvs = sb("wkvs", [P, CH, KVR])
        L.wkr = sb("wkr", [P, CH, NH * RD])
        L.wqa = sb("wqa", [P, NG, HG * QD])
        L.wkvd = sb("wkvd", [KVR, 2, C])
        L.gkv = sb("gkv", [KVR, 1])
        L.wos = sb("wos", [P, CH, C])
        L.wms = sb("wms", [P, CH, C])
        L.wfs = sb("wfs", [P, CH, C])
        L.embd = sb("embd", [P, 4 * NE])
        L.w1s = sb("w1s", [XS, NE, FI], F32R)
        L.w2s = sb("w2s", [P, NE, FD])
        L.b2c = sb("b2c", [P, 4])
        L.bmc = sb("bmc", [P, CH])
        L.bor = sb("bor", [P, C])
        L.cos = sb("cos", [P, NT, RD])
        L.sin = sb("sin", [P, NT, RD])
        L.rank = sb("rank", [P, NE])
        L.mhalf = sb("mhalf", [P, NT])

        L.xs = sb("xs", [P, NT, C])
        L.gate = sb("gate", [P, 2, C])
        L.modc = sb("modc", [P, 4, CH])
        L.stat = sb("stat", [P, NT, 6])
        L.mv = sb("mv", [P, NT, 2])
        L.vare = sb("vare", [P, NT])
        L.rstd = sb("rstd", [P, NT])
        L.ao = sb("ao", [P, NT, C])

        L.ps = root.enter_context(nc.psum_tensor("ps", [P, 8, HALF], F32))

        def bank(n, k=1):
            return L.ps[:, n:n + k, :].rearrange("p b c -> p (b c)")

        L.s_w = sem("s_w")
        L.s_wd = sem("s_wd")
        L.s_ws = sem("s_ws")
        L.s_wm = sem("s_wm")
        L.s_c = sem("s_c")
        L.s_pv = sem("s_pv")
        L.s_pp = sem("s_pp")
        L.s_pa = sem("s_pa")
        L.names_a = ["a_x", "a_mod", "a_st", "a_rstd", "a_xn", "a_tr", "a_ht", "a_lat", "a_latc",
                   "a_sq", "a_ss", "a_r", "a_dec", "a_decc", "a_w", "a_v1"]
        both = ["pr", "t1", "add", "cont", "tr", "hi", "lo", "v", "va", "a", "max", "mf", "mt", "mr", "row",
                "s", "exp", "sel", "pv", "o", "ot", "rs", "ao"]
        L.names_c = [[f"{n}{k}" for n in both] for k in range(2)]
        L.names_d = ["d_tr", "d_at", "d_o", "d_x1", "d_st", "d_rstd", "d_xn", "d_tr2", "d_h2", "d_t",
                   "d_t32", "d_hi", "d_lo", "d_x2", "d_lg", "d_r", "d_e", "d_gt", "d_gtc", "d_one", "d_w"]
        L.names_e = ["e_l1", "e_gelu", "e_l2", "e_gb0", "e_gb1", "e_gb2", "e_gb3", "e_gy", "e_add", "e_cs", "e_ct", "e_o", "e_x2",
                   "e_out", "e_xb"]
        L.S = {n: sem(n) for n in L.names_a + L.names_c[0] + L.names_c[1] + L.names_d + L.names_e}

        def clear(eng, names):
            for n in names:
                eng.sem_clear(L.S[n])

        L.bank, L.clear = bank, clear
        prologue(nc, L)
        for names in (L.names_a, *L.names_c, L.names_d, L.names_e):
            clear(nc.gpsimd, names)
        nc.all_engine_barrier()

        with nc.Fori(0, B) as L.img:
            with ExitStack() as att:
                L.ht = sb("ht", [P, CH, T], F32, att)
                L.qct = sb("qct", [QR, T], F32, att)
                L.kvt = sb("kvt", [KVR, T], F32, att)
                with ExitStack() as tmp:
                    L.xn = sb("xn", [P, NT, C], F32, tmp)
                    L.kvsq = sb("kvsq", [KVR, T], F32, tmp)
                    stage_latents(nc, L)
                L.kst = sb("kst", [P, 4, HG, STK], F32, att)
                L.qst = sb("qst", [P, 4, HG, STK], F32, att)
                L.rot = sb("rot", [P, 2, 2, 2, HG * RD], F32, att)
                L.pt = sb("pt", [P, PTS, HALF], F32, att)
                L.mx = sb("mx", [P, HG * NT, 2], F32, att)
                L.mxf = sb("mxf", [P, HG * NT], F32, att)
                L.mr = sb("mr", [HG * NT, P], F32R, att)
                L.ot = sb("ot", [P, HALF], F32, att)
                L.rs = sb("rs", [P, 4, HG], F32, att)
                L.k2 = [sb(f"k2_{n}", [STK, HG, T], F32R, att) for n in range(2)]
                L.qh = [sb(f"qh_{n}", [STK, HG, T], F32R, att) for n in range(2)]
                L.ql = [sb(f"ql_{n}", [STK, HG, T], F32R, att) for n in range(2)]
                L.va = [sb(f"va_{n}", [P, NT, HG, VW], F32, att) for n in range(2)]
                for turn in range(NG + 1):
                    stage_attend(nc, L, turn)
            with ExitStack() as ffn:
                L.wog = sb("wog", [P, CH, C], F32, ffn)
                L.wfg = sb("wfg", [P, CH, C], F32, ffn)
                L.bog = sb("bog", [P, C], F32, ffn)
                L.gt = sb("gt", [P, T], F32, ffn)
                L.x2 = sb("x2", [XS, FH, T], F32R, ffn)
                with ExitStack() as tmp:
                    L.at = sb("at", [P, CH, T], F32, tmp)
                    L.xn2 = sb("xn2", [P, NT, C], F32, tmp)
                    L.h2t = sb("h2t", [P, CH, T], F32, tmp)
                    L.t32 = sb("t32", [P, CH, T], F32, tmp)
                    L.thi = sb("thi", [P, CH, T], F32R, tmp)
                    L.tlo = sb("tlo", [P, CH, T], F32R, tmp)
                    L.lg = sb("lg", [P, NT * FH, NE], F32, tmp)
                    L.ea = sb("ea", [P, NT * FH, NE], F32, tmp)
                    L.eb = sb("eb", [P, NT * FH, NE], F32, tmp)
                    L.ec = sb("ec", [P, NT * FH, NE], F32, tmp)
                    L.gm = sb("gm", [P, 6, NT * FH], F32, tmp)
                    stage_route(nc, L)
                with ExitStack() as tmp:
                    L.hm = sb("hm", [P, 8, T], F32, tmp)
                    L.gb = sb("gb", [P, 4, T], F32, tmp)
                    L.gy = sb("gy", [P, 3, T], F32, tmp)
                    L.acc = sb("acc", [P, 5, T], F32, tmp)
                    L.ct = sb("ct", [P, CH, T], F32, tmp)
                    L.ob = sb("ob", [P, NT, C], F32, tmp)
                    stage_experts(nc, L)
            clear(nc.gpsimd, L.names_e)
            nc.all_engine_barrier()


def prologue(nc, e):
    with ExitStack() as ctx:
        def sb(name, shape, dt=F32):
            return ctx.enter_context(nc.sbuf_tensor(name, shape, dt))

        w1t = sb("w1t", [XS, NE, FI])
        w1h = sb("w1h", [XS, NE, FI], F32R)
        w1l = sb("w1l", [XS, NE, FI], F32R)
        ct_ = sb("ct_", [P, CH, B])
        cs_ = sb("cs_", [P, CH, B])
        wmo = sb("wmo", [P, CH, 6 * C])
        mrow = sb("mrow", [B, 6 * C])
        g1 = sb("g1", [B, 2, C])
        g2 = sb("g2", [B, 2, C])
        loads = [
            (e.wqs[:, :, :], e.w_q.rearrange("(k p) n -> p k n", p=P)),
            (e.wkvs[:, :, :], e.w_kv.rearrange("(k p) n -> p k n", p=P)),
            (e.wkr[:, :, :], e.w_krope.rearrange("(k p) n -> p k n", p=P)),
            (e.wqa[:, :, 0:HG * RD], e.w_qrope.rearrange("r (g n) -> r g n", g=NG)),
            (e.wqa[:, :, HG * RD:HG * QD], e.w_qdec.rearrange("r (g n) -> r g n", g=NG)),
            (e.wkvd[:, 0, :], e.w_kdec), (e.wkvd[:, 1, :], e.w_vdec),
            (e.gkv[:, :], e.g_kv.rearrange("(p o) -> p o", o=1)),
            (e.wos[:, :, :], e.w_o.rearrange("(k p) n -> p k n", p=P)),
            (e.wms[:, :, :], e.wm.rearrange("(k p) n -> p k n", p=P)),
            (e.wfs[:, :, :], e.wo.rearrange("(k p) n -> p k n", p=P)),
            (e.w2s[:, :, :], e.w2.rearrange("e i o -> i e o")),
            (e.b2c[:, :], e.b2.rearrange("(g e) o -> (e o) g", e=4)),
            (e.bmc[:, :], e.bm.rearrange("(k p) -> p k", p=P)),
            (e.bor[:, :], e.bo.partition_broadcast(P)),
            (e.cos[:, :, :], e.cos_t), (e.sin[:, :, :], e.sin_t),
            (ct_[:, 0, :], e.cvec[:, 0:P].rearrange("b p -> p b")),
            (ct_[:, 1, :], e.cvec[:, P:C].rearrange("b p -> p b")),
            (wmo[:, :, :], e.wmod.rearrange("(k p) n -> p k n", p=P)),
            (w1t[96:97, :, :], e.b1.unsqueeze(0)), (w1t[97:98, :, :], e.b1.unsqueeze(0)),
        ] + [(w1t[FD * k:FD * k + FD, :, :], e.w1.rearrange("e d i -> d e i")) for k in range(3)]
        with nc.Block() as block:
            @block.sync
            def _(sp):
                for dst, src in loads:
                    sp.dma_start(dst, src).then_inc(e.s_w, 16)
                sp.wait_ge(e.s_c, 1)
                for k in range(4):
                    sp.dma_start(e.embd[FD * k:FD * k + FD, NE * k:NE * k + NE], e.emb).then_inc(e.s_wd, 16)
                sp.wait_ge(e.s_pv, 2)
                sp.dma_start(e.w1s[0:32, :, :].bitcast(F32), w1h[0:32, :, :].bitcast(F32)).then_inc(e.s_ws, 16)
                sp.dma_start(e.w1s[32:64, :, :].bitcast(F32), w1l[32:64, :, :].bitcast(F32)).then_inc(e.s_ws, 16)
                sp.dma_start(e.w1s[64:97, :, :].bitcast(F32), w1h[64:97, :, :].bitcast(F32)).then_inc(e.s_ws, 16)
                sp.dma_start(e.w1s[97:98, :, :].bitcast(F32), w1l[97:98, :, :].bitcast(F32)).then_inc(e.s_ws, 16)
                sp.wait_ge(e.s_pv, 12)
                sp.dma_start(e.mod_dram.rearrange("b j c -> b (j c)"), mrow[:, :]).then_inc(e.s_wm, 16)
                sp.wait_ge(e.s_w, 16 * len(loads))
                sp.wait_ge(e.s_wd, 64)
                sp.wait_ge(e.s_ws, 64)
                sp.wait_ge(e.s_wm, 16)

            @block.gpsimd
            def _(g):
                g.memset(e.embd[:, :], 0.0).then_inc(e.s_c, 1)
                g.memset(e.ident[:, :], 0.0).then_inc(e.s_c, 1)
                g.memset(e.maskb[:, :], 0.0).then_inc(e.s_c, 1)
                g.memset(e.ones64[:, :], 1.0).then_inc(e.s_c, 1)
                g.memset(e.mhalf[:, :], -0.5).then_inc(e.s_c, 1)
                for k in range(NE):
                    g.memset(e.rank[:, k:k + 1], float(NE - k)).then_inc(e.s_c, 1)
                g.wait_ge(e.s_c, 3)
                g.affine_select(out=e.ident[:, :], in_=e.ident[:, :], compare_op=ALU.not_equal, fill=1.0,
                                base=0, pattern=[[-1, P]], channel_multiplier=1).then_inc(e.s_c, 1)
                g.affine_select(out=e.maskb[:, :], in_=e.maskb[:, :], compare_op=ALU.is_ge, fill=NEG,
                                base=0, pattern=[[-1, P]], channel_multiplier=1).then_inc(e.s_c, 1)

            consts = 5 + NE + 2

            @block.scalar
            def _(act):
                act.wait_ge(e.s_w, 16 * len(loads))
                nc.scalar.activation(cs_[:, :, :], ct_[:, :, :], ACT.Silu).then_inc(e.s_pa, 1)

            @block.tensor
            def _(pe):
                pe.wait_ge(e.s_pa, 1)
                for n in range(3):
                    for k in range(CH):
                        mm = pe.matmul(e.bank(n)[0:B, :], cs_[:, k, :], wmo[:, k, n * HALF:(n + 1) * HALF],
                                       start=(k == 0), stop=(k == CH - 1))
                mm.then_inc(e.s_pp, 1)

            @block.vector
            def _(v):
                v.wait_ge(e.s_w, 16 * len(loads))
                v.tensor_copy(w1h[:, :, :], w1t[:, :, :]).then_inc(e.s_pv, 1)
                v.wait_ge(e.s_pv, 1)
                v.tensor_tensor(w1l[:, :, :], w1t[:, :, :], w1h[:, :, :].bitcast(F32),
                                ALU.subtract).then_inc(e.s_pv, 1)
                v.tensor_scalar(e.wkvd[:, :, :], e.wkvd[:, :, :], e.gkv[:, 0:1], None, ALU.mult).then_inc(e.s_pv, 1)
                v.wait_ge(e.s_c, consts)
                v.tensor_copy(e.identb[:, :], e.ident[:, :]).then_inc(e.s_pv, 1)
                v.tensor_reduce(e.sum4[:, :], e.ident[:, :].rearrange("p (e o) -> p o e", o=FD), AX.X,
                                ALU.add).then_inc(e.s_pv, 1)
                v.wait_ge(e.s_pp, 1)
                m = mrow[:, :].rearrange("b (j c) -> b j c", c=C)
                v.tensor_copy(mrow[:, :], e.bank(0, 3)[0:B, :]).then_inc(e.s_pv, 1)
                v.wait_ge(e.s_pv, 6)
                v.tensor_scalar(m[:, 1::3, :], m[:, 1::3, :], 1.0, None, ALU.add).then_inc(e.s_pv, 1)
                ga = m[:, 2::3, :]
                v.tensor_scalar(g1[:, :, :], ga, -1.0, None, ALU.mult).then_inc(e.s_pv, 1)
                v.wait_ge(e.s_pv, 8)
                v.tensor_tensor(g2[:, :, :], ga, g1[:, :, :], ALU.max).then_inc(e.s_pv, 1)
                v.wait_ge(e.s_pv, 9)
                v.tensor_scalar(g1[:, :, :], ga, 0.0, 2.0, ALU.is_ge, ALU.mult).then_inc(e.s_pv, 1)
                v.tensor_scalar(g2[:, :, :], g2[:, :, :], 0.25, None, ALU.max).then_inc(e.s_pv, 1)
                v.wait_ge(e.s_pv, 11)
                v.scalar_tensor_tensor(out=ga, in0=g1[:, :, :], scalar=-1.0, in1=g2[:, :, :],
                                       op0=ALU.add, op1=ALU.mult).then_inc(e.s_pv, 1)


def stage_latents(nc, L):
    S, bank, img = L.S, L.bank, L.img
    with nc.Block() as block:
        @block.sync
        def _(sp):
            for c in range(2):
                src = L.x[bass.ds(img, 1)].rearrange("a (t p) c -> p (a t) c", p=P)
                sp.dma_start(L.xs[:, 4 * c:4 * c + 4, :], src[:, 4 * c:4 * c + 4, :]).then_inc(S["a_x"], 16)
            md = L.mod_dram[bass.ds(img, 1)]
            for k, j in enumerate((0, 1, 3, 4)):
                for h in range(CH):
                    sp.dma_start(L.modc[:, k, h:h + 1],
                                 md[:, j, h * P:(h + 1) * P].rearrange("a (p o) -> (a p) o", o=1)
                                 ).then_inc(S["a_mod"], 16)
            for k, j in enumerate((2, 5)):
                sp.dma_start(L.gate[:, k, :], md[:, j, :].broadcast_to([P, C])).then_inc(S["a_mod"], 16)
            sp.wait_ge(S["a_mod"], 160)

        @block.gpsimd
        def _(g):
            g.wait_ge(S["a_st"], 2 * NT + 1)
            g.tensor_tensor(L.rstd[:, :], L.vare[:, :], L.mhalf[:, :], ALU.pow).then_inc(S["a_rstd"], 1)
            g.wait_ge(S["a_r"], 1)
            g.tensor_tensor(L.rstd[:, :], L.vare[:, :], L.mhalf[:, :], ALU.pow).then_inc(S["a_rstd"], 1)

        @block.vector
        def _(v):
            for t in range(NT):
                if t % 4 == 0:
                    v.wait_ge(S["a_x"], 32)
                v.bn_stats(L.stat[:, t, :], L.xs[:, t, :]).then_inc(S["a_st"], 1)
            for t in range(NT):
                v.wait_ge(S["a_st"], t + 1)
                v.bn_aggr(L.mv[:, t, :], L.stat[:, t, :]).then_inc(S["a_st"], 1)
            v.wait_ge(S["a_st"], 2 * NT)
            v.tensor_scalar(L.vare[:, :], L.mv[:, :, 1], EPS_LN, None, ALU.add).then_inc(S["a_st"], 1)
            v.wait_ge(S["a_rstd"], 1)
            for t in range(NT):
                v.tensor_scalar(L.xn[:, t, :], L.xs[:, t, :], L.mv[:, t, 0:1], L.rstd[:, t:t + 1],
                                ALU.subtract, ALU.mult).then_inc(S["a_xn"], 1)
            v.wait_ge(S["a_mod"], 160)
            for c in range(2):
                for j in range(CH):
                    n = CH * c + j
                    v.wait_ge(S["a_tr"], n + 1)
                    v.tensor_scalar(L.ht[:, j, c * HALF:(c + 1) * HALF], bank(n), L.modc[:, 1, j:j + 1],
                                    L.modc[:, 0, j:j + 1], ALU.mult, ALU.add).then_inc(S["a_ht"], 1)
            for c in range(2):
                v.wait_ge(S["a_lat"], 2 * c + 2)
                v.tensor_copy(L.qct[:, c * HALF:(c + 1) * HALF], bank(6 + c)).then_inc(S["a_latc"], 1)
            v.wait_ge(S["a_ss"], 1)
            v.tensor_scalar(L.vare[:, :], bank(0)[:, 0:NT], 1.0 / KVR, EPS_RMS, ALU.mult,
                            ALU.add).then_inc(S["a_r"], 1)

        @block.scalar
        def _(act):
            for c in range(2):
                act.wait_ge(S["a_lat"], 2 * c + 1)
                nc.scalar.copy(L.kvt[:, c * HALF:(c + 1) * HALF], bank(4 + c)[0:KVR, :]).then_inc(S["a_sq"], 1)
                nc.scalar.activation(L.kvsq[:, c * HALF:(c + 1) * HALF], bank(4 + c)[0:KVR, :],
                                     ACT.Square).then_inc(S["a_sq"], 1)

        @block.tensor
        def _(pe):
            for c in range(2):
                for j in range(CH):
                    for t in range(4 * c, 4 * c + 4):
                        pe.wait_ge(S["a_xn"], t + 1)
                        mm = pe.transpose(bank(CH * c + j)[:, (t % 4) * P:(t % 4 + 1) * P],
                                          L.xn[:, t, j * P:(j + 1) * P], L.ident[:, :])
                    mm.then_inc(S["a_tr"], 1)
            for c in range(2):
                pe.wait_ge(S["a_ht"], 2 * c + 2)
                for w, o, m in ((L.wkvs, bank(4 + c)[0:KVR, :], KVR), (L.wqs, bank(6 + c), QR)):
                    for k in range(CH):
                        mm = pe.matmul(o, w[:, k, :], L.ht[:, k, c * HALF:(c + 1) * HALF],
                                       start=(k == 0), stop=(k == CH - 1))
                    mm.then_inc(S["a_lat"], 1)
            pe.wait_ge(S["a_sq"], 4)
            pe.wait_ge(S["a_ht"], 4)
            for t in range(NT):
                mm = pe.matmul(bank(0)[:, t:t + 1], L.kvsq[:, t * P:(t + 1) * P], L.ones64[:, :],
                               start=True, stop=True)
            mm.then_inc(S["a_ss"], 1)


def stage_attend(nc, L, turn):
    bank = L.bank
    S = {n[:-1]: L.S[n] for n in L.names_c[turn % 2]}
    main, side = turn > 0, turn < NG
    cur, nxt = (turn - 1) % 2, turn % 2
    k2, qh, ql, va = L.k2[cur], L.qh[cur], L.ql[cur], L.va[cur]
    k2n, qhn, qln, van = L.k2[nxt], L.qh[nxt], L.ql[nxt], L.va[nxt]
    steps = [(c, j) for c in range(2) for j in range(4 * c + 4)]
    NS = len(steps)
    pairs = {0: [0, 1], 3: [2], 4: [3]}
    quads = {2: [0], 3: [1], 6: [2], 7: [3]}
    rows = {4: [0], 5: [1, 2, 3], 8: [4, 5], 9: [6], 10: [7]}
    LAST = 11
    peaks = [(i, h, n) for i in range(NT) for n in range(i // 4 + 1) for h in range(HG)]

    def first_query(c, j):
        return max(0, j - 4 * c) * P

    def key_range(i, n):
        return slice(n * HALF, min((n + 1) * HALF, (i + 1) * P))

    def stacks_of(n):
        return [4 * m + k for m in quads.get(n, []) for k in range(4)] if side else []

    def peaks_of(n):
        return [k for k in range(len(peaks)) if peaks[k][0] in rows.get(n, [])] if side else []

    PARTS = 4

    def share(work, part):
        return work[len(work) * part // PARTS:len(work) * (part + 1) // PARTS]

    if not side:
        pairs = {}
    diag_before = [sum(HG for (c, j) in steps[:n] if j >= 4 * c) for n in range(NS + 1)]

    def twice(a, n):
        return a.unsqueeze(2).broadcast_to([P, HG, 2, n])

    with nc.Block() as block:
        @block.tensor
        def _(pe):
            freed = []

            def ring(*frees):
                if len(freed) >= 4:
                    for s, n in freed[-4]:
                        pe.wait_ge(s, n)
                freed.append(frees)
                return bank(4 + (len(freed) - 1) % 4)

            def scores(n, heads):
                c, j = steps[n]
                f = first_query(c, j)
                for h in heads:
                    u = HG * n + h
                    if u >= 3:
                        pe.wait_ge(S["exp"], u - 2)
                    q = slice(c * HALF + f, (c + 1) * HALF)
                    key = slice(j * P, (j + 1) * P)
                    pe.matmul(bank(u % 3)[:, 0:HALF - f], k2[:, h, key], qh[:, h, q], start=True, stop=False)
                    pe.matmul(bank(u % 3)[:, 0:HALF - f], k2[:, h, key], ql[:, h, q],
                              start=False, stop=True).then_inc(S["s"], 1)

            def values(n):
                c, j = steps[n]
                f = first_query(c, j)
                pe.wait_ge(S["exp"], HG * (n + 1))
                pe.wait_ge(S["sel"], diag_before[n + 1])
                if (c, j) == (1, 0):
                    pe.wait_ge(S["o"], 1)
                for h in range(HG):
                    mm = pe.matmul(bank(3)[h * VW:(h + 1) * VW, f:HALF], va[:, j, h, :],
                                   L.pt[:, (HG * n + h) % PTS, f:HALF], start=(j == 0), stop=(j == 4 * c + 3))
                mm.then_inc(S["pv"], 1)

            def turn_sums(c):
                pe.wait_ge(S["o"], c + 1)
                out = ring((S["ao"], c + 1))
                for t in range(4):
                    mm = pe.transpose(out[:, t * P:(t + 1) * P], L.ot[:, t * P:(t + 1) * P], L.ident[:, :])
                mm.then_inc(S["ot"], 1)

            def project(p):
                out = ring((S["cont"], 6 * p + 4))
                for t in range(2):
                    tok = slice((2 * p + t) * P, (2 * p + t + 1) * P)
                    for k in range(CH):
                        pe.matmul(out[:, t * P:(t + 1) * P], L.ht[:, k, tok],
                                  L.wkr[:, k, turn * HG * RD:(turn + 1) * HG * RD], start=(k == 0), stop=(k == CH - 1))
                    mm = pe.matmul(out[:, (2 + t) * P:(3 + t) * P], L.kvt[:, tok],
                                   L.wkvd[:, :, turn * HG * HD:(turn + 1) * HG * HD], start=True, stop=True)
                mm.then_inc(S["pr"], 1)
                out = ring((S["cont"], 6 * p + 6))
                for t in range(2):
                    tok = slice((2 * p + t) * P, (2 * p + t + 1) * P)
                    mm = pe.matmul(out[:, t * HG * QD:(t + 1) * HG * QD], L.qct[:, tok], L.wqa[:, turn, :],
                                   start=True, stop=True)
                mm.then_inc(S["pr"], 1)

            def stack(m):
                c, h, isq = m // 8, m % 8 // 2, m % 2
                pe.wait_ge(S["add"], 8 * c + 8)
                pe.wait_ge(S["cont"], 12 * c + 12)
                out = ring((S["lo"], m + 1))
                st = L.qst if isq else L.kst
                for t in range(4):
                    mm = pe.transpose(out[0:STK, t * P:(t + 1) * P], st[:, t, h, :], L.ident[:, :])
                mm.then_inc(S["tr"], 1)

            def peak(k):
                i, h, n = peaks[k]
                pe.wait_ge(S["hi"], 8 * (i // 4 + 1))
                pe.wait_ge(S["lo"], 8 * (i // 4 + 1))
                out = ring((S["max"], k + 1))
                keys = key_range(i, n)
                w = keys.stop - keys.start
                diagonal = keys.stop == (i + 1) * P and n == i // 4
                mm = pe.matmul(out[:, 0:w], qhn[:, h, i * P:(i + 1) * P], k2n[:, h, keys],
                               start=True, stop=not diagonal)
                if diagonal:
                    mm = pe.matmul(out[:, w - P:w], L.identb[:, :], L.maskb[:, :], start=False, stop=True)
                mm.then_inc(S["a"], 1)

            if turn == 0:
                pe.wait_ge(S["v"], 3)
            for n in range(NS + 2):
                if main and n in (6, NS + 1):
                    turn_sums(n // NS)
                for part in range(PARTS):
                    if main and n < NS and part < HG:
                        scores(n, [part])
                    if main and 1 <= n <= NS and part == 2:
                        values(n - 1)
                    for m in share(stacks_of(n), part):
                        stack(m)
                    for k in share(peaks_of(n), part):
                        peak(k)
                    for p in pairs.get(n, []) if part == PARTS - 1 else []:
                        project(p)
                if side:
                    if n == LAST:
                        pe.wait_ge(S["mf"], 1)
                        out = ring((S["mr"], 1))
                        pe.transpose(out[0:HG * NT, 0:P], L.mxf[:, :], L.ident[:, :]).then_inc(S["mt"], 1)

        @block.vector
        def _(v):
            uses = [0]

            def ring():
                uses[0] += 1
                return bank(4 + (uses[0] - 1) % 4)

            def rotate(p):
                for q in range(2):
                    out = ring()
                    w = (HG * RD, HG * QD)[q]
                    v.wait_ge(S["pr"], 2 * p + q + 1)
                    if p:
                        v.wait_ge(S["add"], 4 * (p - 1) + 2 * q + 2)
                    src = out[:, 0:2 * w].rearrange("p (t n) -> p t n", t=2)[:, :, 0:HG * RD]
                    src = src.rearrange("p t (h d) -> p t h d", d=RD)
                    r1, r2 = (L.rot[:, q, k].rearrange("p t (h d) -> p t h d", d=RD) for k in range(2))
                    hd, tt = RD // 2, slice(2 * p, 2 * p + 2)

                    def tab(a, lo, n):
                        return a[:, tt, lo:lo + n].unsqueeze(2).broadcast_to([P, 2, HG, n])

                    v.tensor_tensor(r1, src, tab(L.cos, 0, RD), ALU.mult).then_inc(S["t1"], 1)
                    v.tensor_tensor(r2[:, :, :, 0:hd], src[:, :, :, hd:RD], tab(L.sin, 0, hd),
                                    ALU.mult).then_inc(S["t1"], 1)
                    v.tensor_tensor(r2[:, :, :, hd:RD], src[:, :, :, 0:hd], tab(L.sin, hd, hd),
                                    ALU.mult).then_inc(S["t1"], 1)

            def low(m):
                c, h, isq = m // 8, m % 8 // 2, m % 2
                src, tk = ring(), slice(c * HALF, (c + 1) * HALF)
                v.wait_ge(S["hi"], m + 1)
                if isq:
                    v.tensor_tensor(qln[:, h, tk], src[0:STK, :], qhn[:, h, tk].bitcast(F32),
                                    ALU.subtract).then_inc(S["lo"], 1)
                else:
                    v.tensor_tensor(k2n[LO:STK, h, tk], src[LO:STK, :], k2n[0:QD, h, tk].bitcast(F32),
                                    ALU.subtract).then_inc(S["lo"], 1)

            def largest(k):
                i, h, n = peaks[k]
                keys = key_range(i, n)
                out = ring()
                v.wait_ge(S["a"], k + 1)
                v.tensor_reduce(L.mx[:, h * NT + i, n:n + 1], out[:, 0:keys.stop - keys.start],
                                AX.X, ALU.max).then_inc(S["max"], 1)

            if turn == 0:
                v.memset(L.kst[:, :, :, MROW:LO], 0.0).then_inc(S["v"], 1)
                v.memset(L.qst[:, :, :, MROW:LO], 0.0).then_inc(S["v"], 1)
                v.wait_ge(S["v"], 1)
                v.memset(L.kst[:, :, :, MROW:MROW + 1], -1.0).then_inc(S["v"], 1)
            if side:
                v.memset(L.mx[:, :, 1:2], NEG).then_inc(S["v"], 1)
                v.wait_ge(S["v"], 4 if turn == 0 else 1)

            for n in range(NS + 2):
                if main and n in (5, NS + 1):
                    c = n // NS
                    v.wait_ge(S["pv"], 4 if c == 0 else NS)
                    if c:
                        v.wait_ge(S["ot"], 1)
                    v.tensor_copy(L.ot[:, :], bank(3)).then_inc(S["o"], 1)
                if main and n in (6, NS + 1):
                    c = n // NS
                    src = ring().rearrange("p (t h w) -> p t h w", t=4, w=VW)
                    v.wait_ge(S["ot"], c + 1)
                    v.reciprocal(L.rs[:, :, :], src[:, :, :, HD]).then_inc(S["rs"], 1)
                    v.wait_ge(S["rs"], c + 1)
                    dst = L.ao[:, 4 * c:4 * c + 4, (turn - 1) * HG * HD:turn * HG * HD]
                    v.tensor_tensor(dst.rearrange("p t (h d) -> p t h d", d=HD), src[:, :, :, 0:HD],
                                    L.rs[:, :, :].unsqueeze(3).broadcast_to([P, 4, HG, HD]),
                                    ALU.mult).then_inc(S["ao"], 1)
                if side:
                    for part in range(PARTS):
                        for m in share(stacks_of(n), part):
                            low(m)
                        for k in share(peaks_of(n), part):
                            largest(k)
                    for p in pairs.get(n, []):
                        rotate(p)
                    if n == LAST:
                        v.wait_ge(S["max"], len(peaks))
                        v.tensor_reduce(L.mxf[:, :], L.mx[:, :, :], AX.X, ALU.max).then_inc(S["mf"], 1)
                        out = ring()
                        v.wait_ge(S["mt"], 1)
                        v.tensor_copy(L.mr[:, :], out[0:HG * NT, 0:P]).then_inc(S["mr"], 1)

        @block.sync
        def _(sp):
            if side:
                sp.wait_ge(S["mr"], 1)
                sp.dma_start(qhn[MROW:MROW + 1, :, :].bitcast(F32), L.mr[:, :].bitcast(F32)).then_inc(S["row"], 16)
                sp.wait_ge(S["row"], 16)

        @block.scalar
        def _(act):
            uses = [0]

            def ring():
                uses[0] += 1
                return bank(4 + (uses[0] - 1) % 4)

            def content(p):
                if p == 2:
                    act.wait_ge(S["tr"], 8)
                kv, qq = ring(), ring()
                act.wait_ge(S["t1"], 6 * p + 3)
                for t in range(2):
                    tile = 2 * p + t
                    src = kv[:, (2 + t) * P:(3 + t) * P].rearrange("p (a h d) -> p a h d", a=2, d=HD)
                    dst = L.kst[:, tile % 4, :, 0:LO + QD].rearrange("p h d -> p h d")
                    for u in range(2):
                        ins = nc.scalar.activation(dst[:, :, u * LO + RD:u * LO + QD], src[:, 0], ACT.Copy,
                                                   scale=L.rstd[:, tile:tile + 1])
                    ins.then_inc(S["cont"], 1)
                    nc.scalar.activation(van[:, tile, :, 0:HD], src[:, 1], ACT.Copy,
                                         scale=L.rstd[:, tile:tile + 1]).then_inc(S["cont"], 1)
                act.wait_ge(S["t1"], 6 * p + 6)
                for t in range(2):
                    tile = 2 * p + t
                    o = t * HG * QD + HG * RD
                    src = qq[:, o:o + HG * HD].rearrange("p (h d) -> p h d", d=HD)
                    for u in range(2):
                        ins = nc.scalar.copy(L.qst[:, tile % 4, :, u * LO + RD:u * LO + QD], src)
                    ins.then_inc(S["cont"], 1)

            def high(m):
                c, h, isq = m // 8, m % 8 // 2, m % 2
                src, tk = ring(), slice(c * HALF, (c + 1) * HALF)
                act.wait_ge(S["tr"], m + 1)
                if isq:
                    nc.scalar.copy(qhn[:, h, tk], src[0:STK, :]).then_inc(S["hi"], 1)
                else:
                    nc.scalar.copy(k2n[0:LO, h, tk], src[0:LO, :]).then_inc(S["hi"], 1)

            for n in range(NS + 2):
                if main and n in (6, NS + 1):
                    ring()
                for part in range(PARTS):
                    if main and n < NS:
                        c, j = steps[n]
                        f = first_query(c, j)
                        u = HG * n + part
                        act.wait_ge(S["s"], u + 1)
                        if n >= 2:
                            act.wait_ge(S["pv"], n - 1)
                        nc.scalar.activation(L.pt[:, u % PTS, f:HALF], bank(u % 3)[:, 0:HALF - f], ACT.Exp,
                                             scale=SCALE).then_inc(S["exp"], 1)
                    for m in share(stacks_of(n), part):
                        high(m)
                    for k in share(peaks_of(n), part):
                        ring()
                for p in pairs.get(n, []):
                    content(p)

        @block.gpsimd
        def _(g):
            L.clear(g, L.names_c[(turn - 1) % 2] if turn else L.names_a)
            if turn == 0:
                for k in range(2):
                    g.memset(L.va[k][:, :, :, HD:VW], 0.0).then_inc(S["va"], 1)
                g.wait_ge(S["va"], 2)
                for k in range(2):
                    g.memset(L.va[k][:, :, :, HD:HD + 1], 1.0).then_inc(S["va"], 1)

            def add(p):
                if p == 2:
                    g.wait_ge(S["tr"], 8)
                for q, st in enumerate((L.kst, L.qst)):
                    g.wait_ge(S["t1"], 6 * p + 3 * q + 3)
                    r1, r2 = (L.rot[:, q, k].rearrange("p t (h d) -> p t h d", d=RD) for k in range(2))
                    for t in range(2):
                        dst = bass.AP(st, (2 * p + t) % 4 * HG * STK,
                                      [[4 * HG * STK, P], [STK, HG], [LO, 2], [1, RD]])
                        g.tensor_tensor(dst, twice(r1[:, t], RD), twice(r2[:, t], RD), ALU.add).then_inc(S["add"], 1)

            for n in range(NS + 2):
                if main and n < NS:
                    c, j = steps[n]
                    f = first_query(c, j)
                    if j >= 4 * c:
                        for h in range(HG):
                            g.wait_ge(S["exp"], HG * n + h + 1)
                            blk = L.pt[:, (HG * n + h) % PTS, f:f + P]
                            g.affine_select(out=blk, in_=blk, compare_op=ALU.is_ge, fill=0.0, base=0,
                                            pattern=[[1, P]], channel_multiplier=-1).then_inc(S["sel"], 1)
                if side:
                    for p in pairs.get(n, []):
                        add(p)


def stage_route(nc, L):
    S, bank = L.S, L.bank
    G = NT * FH

    with nc.Block() as block:
        @block.tensor
        def _(pe):
            for c in range(2):
                for j in range(CH):
                    for t in range(4 * c, 4 * c + 4):
                        mm = pe.transpose(bank(CH * c + j)[:, (t % 4) * P:(t % 4 + 1) * P],
                                          L.ao[:, t, j * P:(j + 1) * P], L.ident[:, :])
                    mm.then_inc(S["d_tr"], 1)
            pe.wait_ge(S["d_w"], 5)
            for t in range(NT):
                pe.wait_ge(S["d_at"], 2 * (t // 4) + 2)
                if t >= 4:
                    pe.wait_ge(S["d_x1"], t - 3)
                for k in range(CH):
                    mm = pe.matmul(bank(4 + t % 4)[:, 0:C], L.at[:, k, t * P:(t + 1) * P], L.wog[:, k, :],
                                   start=(k == 0), stop=(k == CH - 1))
                mm.then_inc(S["d_o"], 1)
            for c in range(2):
                for j in range(CH):
                    for t in range(4 * c, 4 * c + 4):
                        pe.wait_ge(S["d_xn"], t + 1)
                        mm = pe.transpose(bank(CH * c + j)[:, (t % 4) * P:(t % 4 + 1) * P],
                                          L.xn2[:, t, j * P:(j + 1) * P], L.ident[:, :])
                    mm.then_inc(S["d_tr2"], 1)
            for c in range(2):
                pe.wait_ge(S["d_h2"], 2 * c + 2)
                for j in range(CH):
                    for k in range(CH):
                        mm = pe.matmul(bank(4 + 2 * c + j), L.wms[:, k, j * P:(j + 1) * P],
                                       L.h2t[:, k, c * HALF:(c + 1) * HALF], start=(k == 0), stop=(k == CH - 1))
                    mm.then_inc(S["d_t"], 1)
            for t in range(NT):
                pe.wait_ge(S["d_t32"], 2 * (t // 4) + 2)
                for j in range(CH):
                    o = (t % 4) * P + j * 4 * NE
                    mm = pe.matmul(bank(t // 4)[:, o:o + 4 * NE], L.t32[:, j, t * P:(t + 1) * P], L.embd[:, :],
                                   start=True, stop=True)
            mm.then_inc(S["d_lg"], 1)
            pe.wait_ge(S["d_r"], 17)
            for t in range(NT):
                mm = pe.transpose(bank(2 + t // 4)[:, (t % 4) * P:(t % 4 + 1) * P],
                                  L.eb[:, t * FH:(t + 1) * FH, :].rearrange("p a b -> p (a b)"), L.ident[:, :])
            mm.then_inc(S["d_gt"], 1)

        @block.vector
        def _(v):
            for k in range(CH):
                v.tensor_tensor(L.wog[:, k, :], L.wos[:, k, :], L.gate[:, 0, :], ALU.mult).then_inc(S["d_w"], 1)
                v.tensor_tensor(L.wfg[:, k, :], L.wfs[:, k, :], L.gate[:, 1, :], ALU.mult).then_inc(S["d_w"], 1)
            v.tensor_tensor(L.bog[:, :], L.bor[:, :], L.gate[:, 1, :], ALU.mult).then_inc(S["d_w"], 1)
            for t in range(NT):
                v.wait_ge(S["d_o"], t + 1)
                v.tensor_tensor(L.xs[:, t, :], bank(4 + t % 4)[:, 0:C], L.xs[:, t, :], ALU.add).then_inc(S["d_x1"], 1)
                v.wait_ge(S["d_x1"], t + 1)
                v.bn_stats(L.stat[:, t, :], L.xs[:, t, :]).then_inc(S["d_st"], 1)
            for t in range(NT):
                v.wait_ge(S["d_st"], NT)
                v.bn_aggr(L.mv[:, t, :], L.stat[:, t, :]).then_inc(S["d_st"], 1)
            v.wait_ge(S["d_st"], 2 * NT)
            v.tensor_scalar(L.vare[:, :], L.mv[:, :, 1], EPS_LN, None, ALU.add).then_inc(S["d_st"], 1)
            v.wait_ge(S["d_rstd"], 1)
            for t in range(NT):
                v.tensor_scalar(L.xn2[:, t, :], L.xs[:, t, :], L.mv[:, t, 0:1], L.rstd[:, t:t + 1],
                                ALU.subtract, ALU.mult).then_inc(S["d_xn"], 1)
            for c in range(2):
                for j in range(CH):
                    n = CH * c + j
                    v.wait_ge(S["d_tr2"], n + 1)
                    v.tensor_scalar(L.h2t[:, j, c * HALF:(c + 1) * HALF], bank(n), L.modc[:, 3, j:j + 1],
                                    L.modc[:, 2, j:j + 1], ALU.mult, ALU.add).then_inc(S["d_h2"], 1)
            for n in range(4):
                c, j = n // 2, n % 2
                v.wait_ge(S["d_t32"], n + 1)
                v.wait_ge(S["d_hi"], n + 1)
                tk = slice(c * HALF, (c + 1) * HALF)
                v.tensor_tensor(L.tlo[:, j, tk], L.t32[:, j, tk], L.thi[:, j, tk].bitcast(F32),
                                ALU.subtract).then_inc(S["d_lo"], 1)
            done = [0]

            def step(ins):
                done[0] += 1
                ins.then_inc(S["d_r"], 1)
                v.wait_ge(S["d_r"], done[0])

            def wide(a):
                return a.unsqueeze(2).broadcast_to([P, G, NE])

            lg, ea, eb, ec = (a[:, :, :] for a in (L.lg, L.ea, L.eb, L.ec))
            rank = L.rank[:, :].unsqueeze(1).broadcast_to([P, G, NE])
            m1, r1, m2, r2, z, rz = (L.gm[:, k, :] for k in range(6))
            v.wait_ge(S["d_lg"], 1)
            step(v.tensor_copy(lg.rearrange("p a b -> p (a b)"), bank(0, 2)))
            step(v.tensor_reduce(m1, lg, AX.X, ALU.max))
            step(v.tensor_tensor(ec, lg, wide(m1), ALU.subtract))
            step(v.tensor_tensor(ea, lg, wide(m1), ALU.is_equal))
            step(v.tensor_tensor(ea, ea, rank, ALU.mult))
            step(v.tensor_reduce(r1, ea, AX.X, ALU.max))
            step(v.tensor_tensor(ea, ea, wide(r1), ALU.is_equal))
            step(v.scalar_tensor_tensor(out=lg, in0=ea, scalar=-3e38, in1=lg, op0=ALU.mult, op1=ALU.add))
            step(v.tensor_reduce(m2, lg, AX.X, ALU.max))
            step(v.tensor_tensor(eb, lg, wide(m2), ALU.is_equal))
            step(v.tensor_tensor(eb, eb, rank, ALU.mult))
            step(v.tensor_reduce(r2, eb, AX.X, ALU.max))
            step(v.tensor_tensor(eb, eb, wide(r2), ALU.is_equal))
            step(v.tensor_tensor(ea, ea, eb, ALU.add))
            v.wait_ge(S["d_e"], 1)
            step(v.tensor_reduce(z, ec, AX.X, ALU.add))
            step(v.reciprocal(rz, z))
            v.tensor_tensor(ea, ea, ec, ALU.mult).then_inc(S["d_st"], 1)
            v.wait_ge(S["d_st"], 2 * NT + 2)
            step(v.tensor_tensor(eb, ea, wide(rz), ALU.mult))
            v.wait_ge(S["d_gt"], 1)
            v.tensor_copy(L.gt[:, :], bank(2, 2)).then_inc(S["d_gtc"], 1)

        @block.scalar
        def _(act):
            for n in range(4):
                c, j = n // 2, n % 2
                act.wait_ge(S["d_tr"], n + 1)
                nc.scalar.copy(L.at[:, j, c * HALF:(c + 1) * HALF], bank(n)).then_inc(S["d_at"], 1)
            for n in range(4):
                c, j = n // 2, n % 2
                act.wait_ge(S["d_t"], n + 1)
                tk = slice(c * HALF, (c + 1) * HALF)
                nc.scalar.activation(L.t32[:, j, tk], bank(4 + n), ACT.Identity,
                                     bias=L.bmc[:, j:j + 1]).then_inc(S["d_t32"], 1)
                act.wait_ge(S["d_t32"], n + 1)
                nc.scalar.copy(L.thi[:, j, tk], L.t32[:, j, tk]).then_inc(S["d_hi"], 1)
            act.wait_ge(S["d_r"], 3)
            nc.scalar.activation(L.ec[:, :, :], L.ec[:, :, :], ACT.Exp).then_inc(S["d_e"], 1)

        @block.gpsimd
        def _(g):
            L.clear(g, L.names_c[NG % 2])
            g.memset(L.x2[3 * FD:XS, :, :].bitcast(F32), 1.0).then_inc(S["d_one"], 1)
            g.wait_ge(S["d_one"], 1)
            g.wait_ge(S["d_st"], 2 * NT + 1)
            g.tensor_tensor(L.rstd[:, :], L.vare[:, :], L.mhalf[:, :], ALU.pow).then_inc(S["d_rstd"], 1)

        @block.sync
        def _(sp):
            for n in range(4):
                c, j = n // 2, n % 2
                tk = slice(c * HALF, (c + 1) * HALF)
                sp.wait_ge(S["d_hi"], n + 1)
                sp.wait_ge(S["d_lo"], n + 1)
                for h in range(4):
                    rows = slice(FD * h, FD * h + FD)
                    for k, src in enumerate((L.thi, L.thi, L.tlo)):
                        sp.dma_start(L.x2[FD * k:FD * k + FD, 4 * j + h, tk].bitcast(F32),
                                     src[rows, j, tk].bitcast(F32)).then_inc(S["d_x2"], 16)
            sp.wait_ge(S["d_x2"], 16 * 48)


def stage_experts(nc, L):
    S, bank = L.S, L.bank
    EG = NE // 4
    NQ = FH * EG
    HM, GB, AC = 8, 4, 5
    EARLY = 18

    with nc.Block() as block:
        @block.tensor
        def _(pe):
            def inner(u):
                h, e = u // NE, u % NE
                if u >= 3:
                    pe.wait_ge(S["e_gelu"], u - 2)
                for c in range(2):
                    mm = pe.matmul(bank(2 * (u % 3) + c), L.w1s[:, e, :], L.x2[:, h, c * HALF:(c + 1) * HALF],
                                   start=True, stop=True)
                mm.then_inc(S["e_l1"], 1)

            def outer(q, c):
                eg = q % EG
                pe.wait_ge(S["e_gelu"], 4 * (q + 1))
                if q:
                    pe.wait_ge(S["e_gy"], 2 * q + c - 1)
                if q == EARLY + 1:
                    pe.wait_ge(S["e_ct"], c + 1)
                for k in range(4):
                    mm = pe.matmul(bank(6 + c)[FD * k:FD * k + FD, :], L.w2s[:, 4 * eg + k, :],
                                   L.hm[:, (4 * q + k) % HM, c * HALF:(c + 1) * HALF], start=True, stop=True)
                mm.then_inc(S["e_l2"], 1)

            def combine(j, q):
                pe.wait_ge(S["e_add"], 12 * (j + 1))
                pe.wait_ge(S["e_gy"], 2 * q + 2)
                for c in range(2):
                    for h in range(4):
                        mm = pe.matmul(bank(6 + c)[FD * h:FD * h + FD, :], L.sum4[:, :],
                                       L.acc[:, (4 * j + h) % AC, c * HALF:(c + 1) * HALF], start=True, stop=True)
                    mm.then_inc(S["e_cs"], 1)

            for u in range(4 * NQ + 5):
                if u < 4 * NQ:
                    inner(u)
                if u >= 6 and u % 4 == 2:
                    outer(u // 4 - 1, 0)
                if u >= 8 and u % 4 == 0:
                    outer(u // 4 - 2, 1)
                    if u // 4 - 2 == EARLY:
                        combine(0, EARLY)
                if u == 4 * NQ:
                    outer(NQ - 1, 0)
                    outer(NQ - 1, 1)
                    break
            combine(1, NQ - 1)
            pe.wait_ge(S["e_ct"], 4)
            for t in range(NT):
                if t >= 6:
                    pe.wait_ge(S["e_x2"], t - 5)
                for k in range(CH):
                    mm = pe.matmul(bank(t % 6)[:, 0:C], L.ct[:, k, t * P:(t + 1) * P], L.wfg[:, k, :],
                                   start=(k == 0), stop=(k == CH - 1))
                mm.then_inc(S["e_o"], 1)

        @block.scalar
        def _(act):
            for u in range(4 * NQ):
                act.wait_ge(S["e_l1"], u + 1)
                if u >= HM:
                    act.wait_ge(S["e_l2"], 2 * (u // 4) - 2)
                nc.scalar.activation(L.hm[:, u % HM, :], bank(2 * (u % 3), 2), ACT.Gelu).then_inc(S["e_gelu"], 1)

        @block.sync
        def _(sp):
            for q in range(NQ):
                if q >= GB:
                    sp.wait_ge(S["e_gy"], 2 * (q - GB) + 2)
                sp.dma_start(L.gb[:, q % GB, :],
                             L.gt[4 * q:4 * q + 4, :].unsqueeze(1).broadcast_to([4, FD, T])
                             ).then_inc(S[f"e_gb{q % GB}"], 16)
            for c in range(2):
                sp.wait_ge(S["e_x2"], 4 * c + 4)
                dst = L.out[bass.ds(L.img, 1)].rearrange("a (t p) c -> p (a t) c", p=P)
                sp.dma_start(dst[:, 4 * c:4 * c + 4, :], L.ob[:, 4 * c:4 * c + 4, :]).then_inc(S["e_out"], 16)
            sp.wait_ge(S["e_out"], 32)

        @block.vector
        def _(v):
            def gated(q, c):
                h, eg = q // EG, q % EG
                v.wait_ge(S["e_l2"], 2 * q + c + 1)
                if c == 0:
                    v.wait_ge(S[f"e_gb{q % GB}"], 16 * (q // GB + 1))
                tk = slice(c * HALF, (c + 1) * HALF)
                if eg == 0:
                    if h >= AC and c == 0:
                        v.wait_ge(S["e_cs"], 2)
                    dst = L.acc[:, h % AC, tk]
                else:
                    if h and c == 0:
                        v.wait_ge(S["e_add"], 3 * h + eg - 3)
                    dst = L.gy[:, eg - 1, tk]
                v.scalar_tensor_tensor(out=dst, in0=bank(6 + c), scalar=L.b2c[:, eg:eg + 1],
                                       in1=L.gb[:, q % GB, tk], op0=ALU.add, op1=ALU.mult).then_inc(S["e_gy"], 1)

            def gathered(j):
                for c in range(2):
                    v.wait_ge(S["e_cs"], 2 * j + c + 1)
                    v.tensor_copy(L.ct[:, j, c * HALF:(c + 1) * HALF], bank(6 + c)).then_inc(S["e_ct"], 1)

            for q in range(NQ):
                gated(q, 0)
                gated(q, 1)
                if q == EARLY:
                    gathered(0)
            gathered(1)
            v.wait_ge(S["e_xb"], 1)
            for t in range(NT):
                v.wait_ge(S["e_o"], t + 1)
                v.tensor_tensor(L.ob[:, t, :], bank(t % 6)[:, 0:C], L.xs[:, t, :], ALU.add).then_inc(S["e_x2"], 1)

        @block.gpsimd
        def _(g):
            L.clear(g, L.names_d)
            g.tensor_tensor(L.xs[:, :, :], L.xs[:, :, :], L.bog[:, :].unsqueeze(1).broadcast_to([P, NT, C]),
                            ALU.add).then_inc(S["e_xb"], 1)
            for h in range(FH):
                for eg in range(1, EG):
                    q = EG * h + eg
                    g.wait_ge(S["e_gy"], 2 * q + 2)
                    if eg > 1:
                        g.wait_ge(S["e_add"], 3 * h + eg - 1)
                    g.tensor_tensor(L.acc[:, h % AC, :], L.acc[:, h % AC, :], L.gy[:, eg - 1, :],
                                    ALU.add).then_inc(S["e_add"], 1)


_INS = {
    "x": "L0_attn_x", "w_kv": "L0_attn_W_kv", "g_kv": "L0_attn_g_kv", "w_kdec": "L0_attn_W_kdec",
    "w_vdec": "L0_attn_W_vdec", "w_q": "L0_attn_W_q", "w_qdec": "L0_attn_W_qdec",
    "w_krope": "L0_attn_W_krope", "w_qrope": "L0_attn_W_qrope", "w_o": "L0_attn_W_o",
    "wm": "L0_ffn_Wm", "bm": "L0_ffn_bm", "emb": "L0_ffn_expert_emb", "w1": "L0_ffn_W1",
    "b1": "L0_ffn_b1", "w2": "L0_ffn_W2", "b2": "L0_ffn_b2", "wo": "L0_ffn_Wo", "bo": "L0_ffn_bo",
    "cvec": "L0_c", "wmod": "L0_wmod",
}


def kernel(**inputs):
    import concourse.bacc as bacc
    from concourse.bass_utils import run_bass_kernel_spmd

    nc = bacc.Bacc("TRN2", target_bir_lowering=False, num_devices=1)
    cos, sin = rope_tables()
    arrays, dram = {}, {}
    for name, a in [(k, np.ascontiguousarray(inputs[n])) for k, n in _INS.items()] + [("cos_t", cos), ("sin_t", sin)]:
        arrays[f"in_{name}"] = a
        dram[name] = nc.dram_tensor(f"in_{name}", a.shape, mybir.dt.from_np(a.dtype), kind="ExternalInput").ap()
    dram["out"] = nc.dram_tensor("out", (B, T, C), F32, kind="ExternalOutput").ap()
    with nc.allow_non_contiguous_dma(reason="small columns of biases and of the modulation"):
        build(nc, dram)
    r = run_bass_kernel_spmd(nc, [arrays], core_ids=[0])
    return r.results[0]["out"]
```
